# Optimizing a Trainium2 kernel written in Bass

```python
import numpy as np
import jax
import jax.numpy as jnp

def _softmax(x, axis=-1):
    return jax.nn.softmax(x, axis=axis)

def _gelu(x):
    return jax.nn.gelu(x, approximate=True)

def _silu(x):
    return jax.nn.silu(x)

def _sigmoid(x):
    return jax.nn.sigmoid(x)

def _layernorm(x, axis=-1, eps=1e-05):
    m = jnp.mean(x, axis=axis, keepdims=True)
    v = jnp.var(x, axis=axis, keepdims=True)
    return (x - m) / jnp.sqrt(v + eps)

def _scatter_add(tgt, idx, src, axis=0):
    return tgt.at[idx].add(src)

def _segment_sum(src, seg, n):
    return jax.ops.segment_sum(src, seg, n)
kernel_name = 'mk_decoder_preln_d1_seqx_r4_1612eb'

def setup_inputs(seed: int=0):
    np.random.seed(seed)
    _w = jnp.asarray

    def _rec_inputs():
        import jax
        import jax.numpy as jnp
        _rk = jax.random.key(seed)
        x = 0.0003765 + 1 * jax.random.normal(jax.random.fold_in(_rk, 1), (16, 256, 512), jnp.float32)
        _lenS = 256 - jax.random.randint(jax.random.fold_in(_rk, 7), (16,), 0, max(1, 256 // 4) + 1, jnp.int32)
        _lenS2 = 256 - jax.random.randint(jax.random.fold_in(_rk, 8), (16,), 0, max(1, 256 // 4) + 1, jnp.int32)
        _ctx_2048P = jax.random.normal(jax.random.fold_in(_rk, 11), (16, 16, 512), jnp.float32)
        _ctx_2048c = jax.random.dirichlet(jax.random.fold_in(_rk, 511), 0.3 * jnp.ones((16,), jnp.float32), (16, 256))
        _ctx_2048t = jnp.einsum('bsk,bkd->bsd', _ctx_2048c, _ctx_2048P)
        _ctx_2048t = _ctx_2048t * jax.lax.rsqrt(jnp.mean(jnp.square(_ctx_2048t)) + 1e-12) * 0.953939
        ctx_2048 = -0.000292821 + 1.00034 * (_ctx_2048t + 0.3 * jax.random.normal(jax.random.fold_in(_rk, 611), (16, 256, 512), jnp.float32))
        return (x, ctx_2048)
    x, ctx_2048 = _rec_inputs()

    def _L0_attn_setup():
        import math
        import jax, jax.numpy as jnp
        import numpy as np
        B, T, E, H = (2, 512, 512, 16)
        D = E // H

        def _alibi_slopes(n):
            start = 2.0 ** (-2.0 ** (-(math.log2(n) - 3)))
            return np.array([start * start ** i for i in range(n)], dtype=np.float32)
        key = jax.random.key(seed)
        ks = jax.random.split(key, 5)
        w_scale = 0.02
        return {'x': jax.random.normal(ks[0], (B, T, E), dtype=jnp.float32), 'Wq': jax.random.normal(ks[1], (E, E), dtype=jnp.float32) * w_scale, 'bq': jnp.zeros((E,), jnp.float32), 'Wk': jax.random.normal(ks[2], (E, E), dtype=jnp.float32) * w_scale, 'bk': jnp.zeros((E,), jnp.float32), 'Wv': jax.random.normal(ks[3], (E, E), dtype=jnp.float32) * w_scale, 'bv': jnp.zeros((E,), jnp.float32), 'Wo': jax.random.normal(ks[4], (E, E), dtype=jnp.float32) * w_scale, 'bo': jnp.zeros((E,), jnp.float32), 'slopes': jnp.asarray(_alibi_slopes(H))}
    _L0_attn_all = _L0_attn_setup()
    _L0_attn_in = {k: v for k, v in _L0_attn_all.items() if k in ('Wq', 'bq', 'Wk', 'bk', 'Wv', 'bv', 'Wo', 'bo', 'slopes')}
    del _L0_attn_all

    def _L0_xattn_setup():
        import jax, jax.numpy as jnp
        import numpy as np
        key = jax.random.key(seed)
        k1, k2, k3, k4, k5 = jax.random.split(key, 5)
        B, D_MODEL, L = (2, 256, 512)
        HEAD_DIM = 8
        H = D_MODEL // HEAD_DIM
        return {'k': jax.random.normal(k1, (B, D_MODEL, L), dtype=jnp.float32), 'v': jax.random.normal(k2, (B, D_MODEL, L), dtype=jnp.float32), 'q': jax.random.normal(k3, (B, D_MODEL, L), dtype=jnp.float32), 'ssm_kernel': jax.random.normal(k4, (H, L), dtype=jnp.float32), 'D': jax.random.normal(k5, (H,), dtype=jnp.float32), 'head_dim': HEAD_DIM}
    _L0_xattn_all = _L0_xattn_setup()
    _L0_xattn_in = {k: v for k, v in _L0_xattn_all.items() if k in ('ssm_kernel', 'D')}
    del _L0_xattn_all

    def _L0_ffn_setup():
        import jax, jax.numpy as jnp
        import numpy as np
        NUM_EXPERTS = 8
        TOP_K = 2
        MODEL_DIM = 512
        INTER_DIM = 256
        GATE_SCALE = 1.0
        UP_SCALE = 0.0
        key = jax.random.key(seed)
        k1, k2, k3, k4 = jax.random.split(key, 4)
        hidden_states = jax.random.normal(k1, (2, 512, MODEL_DIM), jnp.float32)
        router_gate = jax.random.normal(k2, (NUM_EXPERTS, MODEL_DIM), jnp.float32) * 0.02
        expert_gate_up = jax.random.normal(k3, (NUM_EXPERTS, MODEL_DIM, 2 * INTER_DIM), jnp.float32) * 0.02
        expert_down = jax.random.normal(k4, (NUM_EXPERTS, INTER_DIM, MODEL_DIM), jnp.float32) * 0.02
        return {'hidden_states': hidden_states, 'router_gate': router_gate, 'expert_gate_up': expert_gate_up, 'expert_down': expert_down}
    _L0_ffn_all = _L0_ffn_setup()
    _L0_ffn_in = {k: v for k, v in _L0_ffn_all.items() if k in ('router_gate', 'expert_gate_up', 'expert_down')}
    del _L0_ffn_all
    return {'x': x, 'ctx_2048': ctx_2048, 'L0_attn_Wq': _L0_attn_in['Wq'], 'L0_attn_bq': _L0_attn_in['bq'], 'L0_attn_Wk': _L0_attn_in['Wk'], 'L0_attn_bk': _L0_attn_in['bk'], 'L0_attn_Wv': _L0_attn_in['Wv'], 'L0_attn_bv': _L0_attn_in['bv'], 'L0_attn_Wo': _L0_attn_in['Wo'], 'L0_attn_bo': _L0_attn_in['bo'], 'L0_attn_slopes': _L0_attn_in['slopes'], 'L0_xattn_ssm_kernel': _L0_xattn_in['ssm_kernel'], 'L0_xattn_D': _L0_xattn_in['D'], 'L0_ffn_router_gate': _L0_ffn_in['router_gate'], 'L0_ffn_expert_gate_up': _L0_ffn_in['expert_gate_up'], 'L0_ffn_expert_down': _L0_ffn_in['expert_down']}

def reference(x, ctx_2048, L0_attn_Wq, L0_attn_bq, L0_attn_Wk, L0_attn_bk, L0_attn_Wv, L0_attn_bv, L0_attn_Wo, L0_attn_bo, L0_attn_slopes, L0_xattn_ssm_kernel, L0_xattn_D, L0_ffn_router_gate, L0_ffn_expert_gate_up, L0_ffn_expert_down):
    import jax
    import jax.numpy as jnp

    def _L0_attn_ref(x, Wq, bq, Wk, bk, Wv, bv, Wo, bo, slopes):
        import math
        import jax, jax.numpy as jnp
        import numpy as np
        B, T, E, H = (2, 512, 512, 16)
        D = E // H

        def _alibi_slopes(n):
            start = 2.0 ** (-2.0 ** (-(math.log2(n) - 3)))
            return np.array([start * start ** i for i in range(n)], dtype=np.float32)
        b, t, e = x.shape
        h, d = (H, e // H)
        scaling = d ** (-0.5)
        q = (jnp.einsum('bte,fe->btf', x, Wq) + bq) * scaling
        k = jnp.einsum('bte,fe->btf', x, Wk) + bk
        v = jnp.einsum('bte,fe->btf', x, Wv) + bv
        q = q.reshape(b, t, h, d)
        k = k.reshape(b, t, h, d)
        v = v.reshape(b, t, h, d)
        scores = jnp.einsum('bihd,bjhd->bhij', q, k)
        pos = jnp.arange(t)
        alibi = -jnp.abs(pos[None, :] - pos[:, None]).astype(scores.dtype)
        scores = scores + slopes[:, None, None] * alibi
        probs = jax.nn.softmax(scores.astype(jnp.float32), axis=-1).astype(scores.dtype)
        out = jnp.einsum('bhij,bjhd->bihd', probs, v).reshape(b, t, e)
        return jnp.einsum('bte,fe->btf', out, Wo) + bo

    def _L0_xattn_ref(k, v, q, ssm_kernel, D, head_dim):
        import jax, jax.numpy as jnp
        import numpy as np
        B, HD, L = k.shape
        H = HD // head_dim
        fft_size = 2 * L
        k_ = k.reshape(B, H, head_dim, L)
        v_ = v.reshape(B, H, head_dim, L)
        q_ = q.reshape(B, H, head_dim, L)
        kv = jnp.einsum('bhil,bhjl->bijhl', k_, v_)
        kv_f = jnp.fft.rfft(kv, n=fft_size)
        kernel_f = jnp.fft.rfft(ssm_kernel, n=fft_size)
        y = jnp.fft.irfft(kv_f * kernel_f, n=fft_size)[..., :L]
        out = y + kv * D[None, None, None, :, None]
        out = jnp.einsum('bijhl,bhil->bjhl', out, q_)
        out = jnp.transpose(out, (0, 2, 1, 3)).reshape(B, H * head_dim, L)
        return out.astype(k.dtype)

    def _L0_ffn_ref(hidden_states, router_gate, expert_gate_up, expert_down):
        import jax, jax.numpy as jnp
        import numpy as np
        NUM_EXPERTS = 8
        TOP_K = 2
        MODEL_DIM = 512
        INTER_DIM = 256
        GATE_SCALE = 1.0
        UP_SCALE = 0.0
        orig_shape = hidden_states.shape
        hs = hidden_states.reshape(-1, orig_shape[-1])
        T = hs.shape[0]
        logits = hs @ router_gate.T
        probs = jax.nn.softmax(logits.astype(jnp.float32), axis=-1)
        topk_scores, topk_idx = jax.lax.top_k(probs, TOP_K)
        topk_scores = topk_scores / jnp.sum(topk_scores, axis=-1, keepdims=True)
        scores_f = topk_scores.T.reshape(-1).astype(hs.dtype)
        ids_f = topk_idx.T.reshape(-1)
        order = jnp.argsort(ids_f)
        sorted_ids = ids_f[order]
        scores_sorted = scores_f[order]
        token_slots = order % T
        x = hs[token_slots]
        inter = jnp.zeros((x.shape[0], 2 * INTER_DIM), x.dtype)
        for e in range(NUM_EXPERTS):
            m = (sorted_ids == e)[:, None]
            inter = inter + jnp.where(m, x, 0) @ expert_gate_up[e]
        gate = inter[..., 0::2]
        up = inter[..., 1::2]
        h = (up + UP_SCALE) * jax.nn.silu(gate * GATE_SCALE)
        out_rows = jnp.zeros((x.shape[0], MODEL_DIM), x.dtype)
        for e in range(NUM_EXPERTS):
            m = (sorted_ids == e)[:, None]
            out_rows = out_rows + jnp.where(m, h, 0) @ expert_down[e]
        out = jnp.zeros_like(hs).at[token_slots].add(out_rows * scores_sorted[:, None])
        return out.reshape(orig_shape)
    x = x + _L0_attn_ref(_layernorm(x, axis=-1), L0_attn_Wq, L0_attn_bq, L0_attn_Wk, L0_attn_bk, L0_attn_Wv, L0_attn_bv, L0_attn_Wo, L0_attn_bo, L0_attn_slopes)
    x = x + _L0_xattn_ref(ctx_2048, ctx_2048, _layernorm(x, axis=-1), L0_xattn_ssm_kernel, L0_xattn_D, 8)
    x = x + _L0_ffn_ref(_layernorm(x, axis=-1), L0_ffn_router_gate, L0_ffn_expert_gate_up, L0_ffn_expert_down)
    return x

_drawn_inputs = setup_inputs


def setup_inputs(seed=0):
    import zlib

    import numpy as np

    out = dict(_drawn_inputs(seed))
    spreads = {'L0_attn_bq': (0.0, 0.8),
     'L0_attn_bk': (0.0, 0.8),
     'L0_attn_bv': (0.0, 0.1),
     'L0_attn_bo': (0.0, 0.1)}
    factors = {'L0_attn_Wq': 7.161,
     'L0_attn_Wk': 6.662,
     'L0_ffn_router_gate': 8.0,
     'L0_ffn_expert_gate_up': 8.0,
     'L0_ffn_expert_down': 8.0}
    for name, (base, spread) in spreads.items():
        noise = np.random.default_rng([zlib.crc32(name.encode()), seed]).standard_normal(out[name].shape)
        drawn = base * np.exp(spread * noise) if base else spread * noise
        out[name] = jnp.asarray(drawn.astype(out[name].dtype))
    for name, factor in factors.items():
        out[name] = (out[name] * factor).astype(out[name].dtype)
    return out
```

```python
from contextlib import ExitStack

import concourse.bass as bass
from concourse import mybir

F32 = mybir.dt.float32
F32R = mybir.dt.float32r
BF16 = mybir.dt.bfloat16
I32 = mybir.dt.int32
U32 = mybir.dt.uint32
ALU = mybir.AluOpType
ACT = mybir.ActivationFunctionType
AX_X = mybir.AxisListType.X

P = 128
EPS = 1e-5
ds = bass.ds
RSQRT_MAGIC = 1597463007.0
NEWTON_STEPS = 3
RSTD_OPS = 1 + 4 * NEWTON_STEPS


def wait_apart(engine, semaphore, value, passed):
    engine.wait_ge(semaphore, value)
    engine.sem_inc(passed, 1)


def reciprocal_sqrt(pool, out, variance, var_eps, scratch, step, count, done, passed):
    pool.tensor_scalar(var_eps, variance, EPS, None, ALU.add).then_inc(step, 1)
    wait_apart(pool, step, count + 1, passed)
    pool.tensor_scalar(out.bitcast(I32), var_eps.bitcast(I32), -0.5, RSQRT_MAGIC, ALU.mult, ALU.add).then_inc(step, 1)
    n = 2
    for i in range(NEWTON_STEPS):
        wait_apart(pool, step, count + n, passed)
        pool.tensor_tensor(scratch, var_eps, out, ALU.mult).then_inc(step, 1)
        wait_apart(pool, step, count + (n + 1), passed)
        pool.tensor_tensor(scratch, scratch, out, ALU.mult).then_inc(step, 1)
        wait_apart(pool, step, count + (n + 2), passed)
        pool.tensor_scalar(scratch, scratch, -0.5, 1.5, ALU.mult, ALU.add).then_inc(step, 1)
        wait_apart(pool, step, count + (n + 3), passed)
        last = pool.tensor_tensor(out, out, scratch, ALU.mult)
        n += 4
        if i < NEWTON_STEPS - 1:
            last.then_inc(step, 1)
    last.then_inc(done, 1)


def build_decoder(nc, x, ctx_t, wq_t, bq, wk_t, bk, wv_t, bv, wo_t, bo, slopes,
                  ssm_kernel, ssm_d, router_t, gate_up, down, out):
    B, T, E = x.shape
    H = slopes.shape[0]
    DH = E // H
    TT = T // P
    EC = E // P
    NT = B * TT
    HPC = P // DH
    Q_SCALE = DH ** -0.5
    SH = ssm_kernel.shape[0]
    SD = T // SH
    NE = router_t.shape[1]
    FI = down.shape[1]
    assert TT == 2 and EC == 4 and HPC == 4 and H == 16 and SD == 8 and B % 2 == 0

    x_tiles = x.rearrange("b (t p) e -> p (b t) e", p=P)
    out_tiles = out.rearrange("b (t p) e -> p (b t) e", p=P)

    with ExitStack() as whole:
        def sem(name):
            return whole.enter_context(nc.semaphore(name))

        def sbuf(name, shape, dt=F32, scope=whole):
            return scope.enter_context(nc.sbuf_tensor(name, shape, dt))

        def psum(name, shape, scope):
            return scope.enter_context(nc.psum_tensor(name, shape, F32))

        passed = sem("passed")
        ident = sbuf("ident", [P, P])
        all_stats = sbuf("all_stats", [P, NT, 6])
        all_moments = sbuf("all_moments", [P, NT, 2])
        all_rstd = sbuf("all_rstd", [P, NT])
        var_eps = sbuf("var_eps", [P, NT])
        newton = sbuf("newton", [P, NT])
        x1_rows = nc.dram_tensor("x1_rows", [B * T, E], F32)
        x1_tiles = x1_rows.rearrange("(n p) e -> p n e", p=P)
        kernel_pad = nc.dram_tensor("kernel_pad", [SH, P + E], F32)

        N_TOK = B * T
        TOP = 2
        N_TILES = TOP * N_TOK // P + NE
        TOKEN, BACK, SCORE, PAIR_ROW = 0, 1, 2, 4
        NO_ROW = 1.0e6
        TABLE_ROWS = NE * N_TOK + NE * P
        row_table = nc.dram_tensor("row_table", [TABLE_ROWS, PAIR_ROW], F32)
        xn_rows = nc.dram_tensor("xn_rows", [N_TOK, E], F32)
        expert_out = nc.dram_tensor("expert_out", [TOP * N_TOK, E], F32)

        with ExitStack() as scope:
            def sb(name, shape, dt=F32):
                return sbuf(name, shape, dt, scope)

            stats = sb("stats", [P, TT, 6])
            moments = sb("moments", [P, TT, 2])
            rstd = sb("rstd", [P, TT])
            xn = sb("xn", [P, TT, E])
            x_in = [sb(f"x_in{i}", [P, TT, E]) for i in range(2)]
            x_mid = [sb(f"x_mid{i}", [P, TT, E]) for i in range(2)]
            WEIGHT_BUFS = 2
            w_in = [sb(f"w_in{i}", [P, 2, E]) for i in range(WEIGHT_BUFS)]
            wq, wk, wv, wo = [[sb(f"{name}_{part}", [P, EC, E], F32R) for part in ("hi", "lo")]
                              for name in ("wq", "wk", "wv", "wo")]
            bq_col = sb("bq_col", [P, EC])
            bk_col = sb("bk_col", [P, EC])
            bv_row = sb("bv_row", [P, E])
            bo_row = sb("bo_row", [P, E])
            slope_row = sb("slope_row", [P, H])
            slope_scaled = sb("slope_scaled", [P, H])
            dist_i = sb("dist_i", [P, T + P], I32)
            dist = sb("dist", [P, T + P])
            dist_neg = sb("dist_neg", [P, T + P])
            alibi = [sb(f"alibi{i}", [P, T + P]) for i in range(2)]
            kernel_row = sb("kernel_row", [SH, P + E])
            free_rows = sb("free_rows", [P, TABLE_ROWS // P, PAIR_ROW])
            d_col = sb("d_col", [SH, 1])
            xn_t = [sb(f"xn_t_{part}", [P, EC, T], F32R) for part in ("hi", "lo")]
            q_hi, q_lo, k_hi, k_lo = [sb(name, [P, EC, T], F32R) for name in ("q_hi", "q_lo", "k_hi", "k_lo")]
            q_stack = sb("q_stack", [3 * DH, HPC, EC, T], F32R)
            k_stack = sb("k_stack", [3 * DH, HPC, EC, T], F32R)
            v = [sb(f"v{i}", [P, TT, E]) for i in range(2)]
            neg_scores = [sb(f"neg_scores{i}", [P, TT, T]) for i in range(2)]
            probs = [sb(f"probs{i}", [P, TT, T]) for i in range(2)]
            probs_t = [sb(f"probs_t{i}", [P, TT, T]) for i in range(2)]
            neg_max = [sb(f"neg_max{i}", [P, H, TT]) for i in range(2)]
            row_sum = [sb(f"row_sum{i}", [P, TT, H]) for i in range(2)]
            inv_sum = sb("inv_sum", [P, TT, H])
            o_norm = sb("o_norm", [P, TT, E])
            o_t = [sb(f"o_t_{part}", [P, EC, T], F32R) for part in ("hi", "lo")]

            ps_scores = [psum(f"ps_scores{i}", [P, TT, T], scope) for i in range(2)]
            ps_probs_t = [psum(f"ps_probs_t{i}", [P, TT, T], scope) for i in range(2)]
            ps_o = psum("ps_o", [P, TT, E], scope)
            ps_proj = psum("ps_proj", [P, 2, E], scope)

            x_load = [sem(f"x_load{i}") for i in range(2)]
            x1_stored = [sem(f"x1_stored{i}") for i in range(2)]
            stack_load = [sem(f"stack_load{r}") for r in range(HPC)]
            w_load = [sem(f"w_in_load{i}") for i in range(WEIGHT_BUFS)]
            w_hi_ready = sem("w_hi_ready")
            w_ready = sem("w_ready")
            small_load = sem("small_load")
            kernel_store = sem("kernel_store")
            free_row_step = sem("free_row_step")
            free_rows_store = sem("free_rows_store")
            consts = sem("consts")
            alibi_step = sem("alibi_step")
            alibi_ready = sem("alibi_ready")
            kernel_ready = sem("kernel_ready")
            stats_ready = sem("stats_ready")
            moments_ready = sem("moments_ready")
            rstd_ready = sem("rstd_ready")
            rstd_step = sem("rstd_step")
            xn_ready = sem("xn_ready")
            bias_added = sem("bias_added")
            xt_done = sem("xt_done")
            xt_kept = sem("xt_kept")
            q_done = sem("q_done")
            q_kept = sem("q_kept")
            k_done = sem("k_done")
            k_kept = sem("k_kept")
            v_done = sem("v_done")
            v_kept = sem("v_kept")
            ot_done = sem("ot_done")
            ot_kept = sem("ot_kept")
            wo_done = sem("wo_done")
            x1_ready = sem("x1_ready")
            x1_stats = sem("x1_stats")
            scores_ready = sem("scores_ready")
            max_ready = sem("max_ready")
            probs_ready = sem("probs_ready")
            probs_t_ready = sem("probs_t_ready")
            probs_t_kept = [sem(f"probs_t_kept{i}") for i in range(2)]
            pv_ready = sem("pv_ready")
            inv_ready = sem("inv_ready")
            o_kept = sem("o_kept")

            def after(k, par):
                return (k, 1) if par == 0 else (k + 1, 0)

            def before(k, par):
                return (k, 0) if par == 1 else (k - 1, 1)

            def batch(k, par):
                return k * 2 + par

            def head(k, par, h):
                return k * (2 * H) + (par * H + h)

            HEADS = [c * HPC + r for r in range(HPC) for c in range(EC)]
            O_SLOTS, Q_SLOTS, K_SLOTS, V_SLOTS = (2, 2, 3, 4), (5, 6, 6, 7), (8, 8, 9, 10), (11, 12, 13, 14)
            VECTOR_HEADS = (1, 5, 9, 13)
            STACK_LOADS = 6 * 16

            def is_first(k, par, h=0):
                return isinstance(k, int) and k == 0 and par == 0 and h < 2

            def steps(eng, emit):
                emit(0, 0, False, True)
                with eng.Fori(0, B // 2 - 1) as k:
                    emit(k, 1, True, True)
                    emit(k + 1, 0, True, True)
                emit(B // 2 - 1, 1, True, False)

            block = scope.enter_context(nc.Block())

            @block.sync
            def _(sp):
                def load_x(k, par):
                    b = batch(k, par)
                    if not (isinstance(k, int) and k == 0):
                        sp.wait_ge(xn_ready, b * TT - TT)
                        sp.wait_ge(bias_added, b * TT - TT)
                    sp.dma_start(x_in[par][:], x_tiles[:, ds(b * TT, TT), :]).then_inc(x_load[par], 16)

                def store_x1(k, par):
                    b = batch(k, par)
                    sp.wait_ge(x1_ready, b * TT + TT)
                    sp.dma_start(x1_tiles[:, ds(b * TT, TT), :], x_mid[par][:]).then_inc(x1_stored[par], 16)

                load_x(0, 0)
                n = 0
                for src in (wq_t, wk_t, wv_t, wo_t):
                    for half in range(2):
                        if n >= WEIGHT_BUFS:
                            sp.wait_ge(w_ready, n + 1 - WEIGHT_BUFS)
                        sp.dma_start(w_in[n % WEIGHT_BUFS][:],
                                     src.rearrange("(h c p) f -> h p c f", h=2, p=P)[half]).then_inc(w_load[n % WEIGHT_BUFS], 16)
                        n += 1
                load_x(0, 1)
                load_x(1, 0)
                load_x(1, 1)
                sp.wait_ge(free_row_step, 2)
                sp.dma_start(row_table.rearrange("(p k) c -> p k c", p=P), free_rows[:]).then_inc(free_rows_store, 16)
                sp.wait_ge(kernel_ready, 3)
                sp.dma_start(kernel_pad[:, :], kernel_row[:]).then_inc(kernel_store, 16)
                with sp.Fori(2, B // 2) as k:
                    for par in range(2):
                        store_x1(k - 2, par)
                        load_x(k, par)
                for k in (B // 2 - 2, B // 2 - 1):
                    for par in range(2):
                        store_x1(k, par)
                for par in range(2):
                    sp.wait_ge(x1_stored[par], B // 2 * 16)
                sp.wait_ge(kernel_store, 16)
                sp.wait_ge(free_rows_store, 16)

            @block.gpsimd
            def _(pool):
                for dst, src in ((bq_col, bq), (bk_col, bk)):
                    pool.dma_start(dst[:], src).then_inc(small_load, 16)
                for dst, src in ((bv_row, bv), (bo_row, bo), (slope_row, slopes)):
                    pool.dma_start(dst[:], src.partition_broadcast(P)).then_inc(small_load, 16)
                pool.dma_start(d_col[:], ssm_d.rearrange("(h o) -> h o", o=1)).then_inc(small_load, 16)
                pool.dma_start(kernel_row[:, P:], ssm_kernel).then_inc(small_load, 16)
                pool.memset(ident[:], 0.0).then_inc(consts, 1)
                pool.wait_ge(consts, 1)
                pool.affine_select(out=ident[:], in_=ident[:], compare_op=ALU.not_equal, fill=1.0, base=0,
                                   pattern=[[-1, P]], channel_multiplier=1).then_inc(consts, 1)
                pool.iota(dist_i[:], pattern=[[-1, T + P]], base=P, channel_multiplier=1).then_inc(consts, 1)
                pool.memset(kernel_row[:, 0:P], 0.0).then_inc(kernel_ready, 1)
                pool.memset(free_rows[:], 0.0).then_inc(free_row_step, 1)
                pool.wait_ge(free_row_step, 1)
                pool.memset(free_rows[:, :, BACK:BACK + 1], NO_ROW).then_inc(free_row_step, 1)

                def rstd_of(k, par):
                    wait_apart(pool, moments_ready, batch(k, par) * TT + TT, passed)
                    reciprocal_sqrt(pool, rstd[:], moments[:, :, 1], var_eps[:, 0:TT], newton[:, 0:TT], rstd_step,
                                    batch(k, par) * RSTD_OPS, rstd_ready, passed)

                def add_output_bias(k, par):
                    b = batch(k, par)
                    pool.wait_ge(small_load, 16 * 7)
                    wait_apart(pool, xn_ready, b * TT + TT, passed)
                    if not (isinstance(k, int) and k == 0):
                        wait_apart(pool, x1_stored[par], k * 16, passed)
                        wait_apart(pool, x1_stats, b * TT - TT, passed)
                    for tt in range(TT):
                        pool.tensor_tensor(x_mid[par][:, tt, :], x_in[par][:, tt, :], bo_row[:], ALU.add)\
                            .then_inc(bias_added, 1)

                def stack(k, par, r, q_part):
                    b = batch(k, par)
                    wait_apart(pool, q_kept if q_part else k_kept, b * (2 * EC) + 2 * EC, passed)
                    if not is_first(k, par):
                        wait_apart(pool, scores_ready, head(k, par, r * EC) + EC - H, passed)
                    to, parts = (q_stack, (q_hi, q_lo, q_hi)) if q_part else (k_stack, (k_hi, k_hi, k_lo))
                    for n, part in enumerate(parts):
                        pool.dma_start(to[n * DH:n * DH + DH, r, :, :], part[r * DH:r * DH + DH, :, :])\
                            .then_inc(stack_load[r], 16)

                STACK_ORDER = [(0, True), (1, True), (2, True), (0, False), (1, False), (2, False), (3, True), (3, False)]
                STACK_SLOTS = (8, 9, 10, 11, 12, 13, 14, 15)

                rstd_of(0, 0)
                add_output_bias(0, 0)
                for r in range(HPC):
                    for q_part in (True, False):
                        stack(0, 0, r, q_part)

                def step(k, par, has_before, has_after):
                    for i in range(H):
                        if has_after and i == 1:
                            rstd_of(*after(k, par))
                        if has_after and i == 7:
                            add_output_bias(*after(k, par))
                        if has_after and i in STACK_SLOTS:
                            stack(*after(k, par), *STACK_ORDER[STACK_SLOTS.index(i)])

                steps(pool, step)

            @block.tensor
            def _(pe):
                def x_transposes(k, par, bank_read, read):
                    b = batch(k, par)
                    pe.wait_ge(xn_ready, b * TT + TT)
                    for half in range(2):
                        if bank_read is not None:
                            pe.wait_ge(bank_read, read + half)
                        for c in range(2):
                            for tt in range(TT):
                                e = 2 * half + c
                                last = pe.transpose(ps_proj[:, half, c * T + tt * P:c * T + tt * P + P],
                                                    xn[:, tt, e * P:e * P + P], ident[:])
                        last.then_inc(xt_done, 1)

                PARTS = ((0, 0), (0, 1), (1, 0))

                def q_or_k(k, par, half, c, w, done):
                    b = batch(k, par)
                    if c == 0 and w is wq:
                        pe.wait_ge(xt_kept, b * 4 + 4)
                    elif c == 0:
                        pe.wait_ge(q_kept, b * (2 * EC) + (4 * half + 4))
                    f = 2 * half + c
                    for e in range(EC):
                        for w_part, x_part in PARTS:
                            last = pe.matmul(ps_proj[:, half, c * T:c * T + T], w[w_part][:, e, f * P:f * P + P],
                                             xn_t[x_part][:, e, :], start=(e == 0 and w_part == x_part == 0),
                                             stop=(e == EC - 1 and w_part == 1))
                    if c == 1:
                        last.then_inc(done, 1)

                def token_rows(rows, w, tt, piece):
                    for e in (2 * piece, 2 * piece + 1):
                        for x_part, w_part in PARTS:
                            last = pe.matmul(ps_proj[:, tt, :], rows[x_part][:, e, tt * P:tt * P + P], w[w_part][:, e, :],
                                             start=(e == 0 and w_part == x_part == 0),
                                             stop=(e == EC - 1 and x_part == 1))
                    return last

                def v_rows(k, par, tt, piece):
                    if piece == 0:
                        pe.wait_ge(k_kept, batch(k, par) * (2 * EC) + (4 * tt + 4))
                    last = token_rows(xn_t, wv, tt, piece)
                    if piece == 1:
                        last.then_inc(v_done, 1)

                def o_transposes(k, par, v_read):
                    pe.wait_ge(o_kept, batch(k, par) * TT + TT)
                    for half in range(2):
                        if v_read is not None:
                            pe.wait_ge(v_kept, v_read + half)
                        for c in range(2):
                            for tt in range(TT):
                                e = 2 * half + c
                                last = pe.transpose(ps_proj[:, half, c * T + tt * P:c * T + tt * P + P],
                                                    o_norm[:, tt, e * P:e * P + P], ident[:])
                        last.then_inc(ot_done, 1)

                def output_rows(k, par, tt, piece):
                    if piece == 0:
                        pe.wait_ge(ot_kept, batch(k, par) * 4 + 4)
                    last = token_rows(o_t, wo, tt, piece)
                    if piece == 1:
                        last.then_inc(wo_done, 1)

                def scores(k, par, h):
                    b = batch(k, par)
                    r, c = h // EC, h % EC
                    if c == 0:
                        pe.wait_ge(stack_load[r], b * STACK_LOADS + STACK_LOADS)
                    if not is_first(k, par, h):
                        pe.wait_ge(max_ready, head(k, par, h) - 1)
                    for tt in range(TT):
                        last = pe.matmul(ps_scores[h % 2][:, tt, :], q_stack[:, r, c, tt * P:tt * P + P],
                                         k_stack[:, r, c, :], start=True, stop=True)
                    last.then_inc(scores_ready, 1)

                def probs_transposes(k, par, h):
                    pe.wait_ge(probs_ready, head(k, par, h) + 1)
                    if not is_first(k, par, h):
                        pe.wait_ge(probs_t_kept[h % 2], batch(k, par) * (H // 2) + h // 2)
                    for jt in range(TT):
                        for tt in range(TT):
                            last = pe.transpose(ps_probs_t[h % 2][:, jt, tt * P:tt * P + P],
                                                probs[h % 2][:, tt, jt * P:jt * P + P], ident[:])
                    last.then_inc(probs_t_ready, 1)

                def pv(k, par, h):
                    b = batch(k, par)
                    if h == 0:
                        pe.wait_ge(v_kept, b * TT + TT)
                        if not is_first(k, par):
                            pe.wait_ge(o_kept, b * TT)
                    pe.wait_ge(probs_t_kept[h % 2], b * (H // 2) + (h // 2 + 1))
                    features = slice(HEADS[h] * DH, HEADS[h] * DH + DH)
                    for tt in range(TT):
                        for jt in range(TT):
                            last = pe.matmul(ps_o[:, tt, features], probs_t[h % 2][:, jt, tt * P:tt * P + P],
                                             v[par][:, jt, features], start=(jt == 0), stop=(jt == TT - 1))
                    last.then_inc(pv_ready, 1)

                def step(k, par, has_before, has_after):
                    b, prev, nxt = batch(k, par), before(k, par), after(k, par)
                    for h in range(H):
                        if h + 2 < H:
                            scores(k, par, h + 2)
                        elif has_after:
                            scores(*nxt, h + 2 - H)
                        if has_before and h == 1:
                            o_transposes(*prev, b * TT + 1)
                        for n, slot in enumerate(O_SLOTS):
                            if has_before and h == slot:
                                output_rows(*prev, n // 2, n % 2)
                        if has_after and h == O_SLOTS[-1]:
                            if has_before:
                                x_transposes(*nxt, x1_ready, b * TT - TT + 1)
                            else:
                                x_transposes(*nxt, v_kept, 1)
                        if has_after:
                            for n in range(4):
                                if h == Q_SLOTS[n]:
                                    q_or_k(*nxt, n // 2, n % 2, wq, q_done)
                                if h == K_SLOTS[n]:
                                    q_or_k(*nxt, n // 2, n % 2, wk, k_done)
                                if h == V_SLOTS[n]:
                                    v_rows(*nxt, n // 2, n % 2)
                        probs_transposes(k, par, h)
                        if h:
                            pv(k, par, h - 1)
                        elif has_before:
                            pv(*prev, H - 1)

                pe.wait_ge(consts, 2)
                x_transposes(0, 0, None, 0)
                for w, done, halves in ((wq, q_done, 2), (wk, k_done, 4)):
                    pe.wait_ge(w_ready, halves)
                    for n in range(4):
                        q_or_k(0, 0, n // 2, n % 2, w, done)
                pe.wait_ge(w_ready, 8)
                for n in range(4):
                    v_rows(0, 0, n // 2, n % 2)
                scores(0, 0, 0)
                scores(0, 0, 1)
                steps(pe, step)
                pv(B // 2 - 1, 1, H - 1)
                o_transposes(B // 2 - 1, 1, None)
                for n in range(4):
                    output_rows(B // 2 - 1, 1, n // 2, n % 2)

            @block.vector
            def _(dve):
                def token_stats(k, par):
                    dve.wait_ge(x_load[par], k * 16 + 16)
                    for tt in range(TT):
                        dve.bn_stats(stats[:, tt, :], x_in[par][:, tt, :]).then_inc(stats_ready, 1)

                def token_moments(k, par):
                    wait_apart(dve, stats_ready, batch(k, par) * TT + TT, passed)
                    for tt in range(TT):
                        dve.bn_aggr(moments[:, tt, :], stats[:, tt, :]).then_inc(moments_ready, 1)

                def normalise(k, par, tt):
                    dve.wait_ge(rstd_ready, batch(k, par) + 1)
                    dve.tensor_scalar(xn[:, tt, :], x_in[par][:, tt, :], moments[:, tt, 0:1], rstd[:, tt:tt + 1],
                                      ALU.subtract, ALU.mult).then_inc(xn_ready, 1)

                def keep_t_lo(k, par, to, kept):
                    for half in range(2):
                        dve.wait_ge(kept, batch(k, par) * 4 + (2 * half + 1))
                        dve.tensor_tensor(to[1][:, 2 * half:2 * half + 2, :],
                                          ps_proj[:, half, :].rearrange("p (c t) -> p c t", t=T),
                                          to[0][:, 2 * half:2 * half + 2, :], ALU.subtract).then_inc(kept, 1)

                def keep_q_lo(k, par, half):
                    n = batch(k, par) * (2 * EC) + half * 4
                    for c in range(2):
                        f = 2 * half + c
                        dve.wait_ge(q_kept, n + (2 + c))
                        dve.scalar_tensor_tensor(q_lo[:, f, :], ps_proj[:, half, c * T:c * T + T], bq_col[:, f:f + 1],
                                                 q_hi[:, f, :], ALU.add, ALU.subtract).then_inc(q_kept, 1)

                def keep_k_lo(k, par, half):
                    n = batch(k, par) * (2 * EC) + half * 4
                    for c in range(2):
                        f = 2 * half + c
                        dve.wait_ge(k_kept, n + (2 + c))
                        dve.scalar_tensor_tensor(k_lo[:, f, :], ps_proj[:, half, c * T:c * T + T], bk_col[:, f:f + 1],
                                                 k_hi[:, f, :], ALU.add, ALU.subtract).then_inc(k_kept, 1)

                def keep_v(k, par, tt):
                    dve.wait_ge(v_done, batch(k, par) * TT + (tt + 1))
                    dve.tensor_tensor(v[par][:, tt, :], ps_proj[:, tt, :], bv_row[:], ALU.add).then_inc(v_kept, 1)

                def head_alibi(k, par, h):
                    if not is_first(k, par, h):
                        dve.wait_ge(max_ready, head(k, par, h) - 1)
                    dve.tensor_scalar(alibi[h % 2][:], dist_neg[:], slope_scaled[:, HEADS[h]:HEADS[h] + 1], None,
                                      ALU.mult).then_inc(alibi_ready, 1)

                def score_max(k, par, h):
                    g = head(k, par, h)
                    if not is_first(k, par, h):
                        dve.wait_ge(probs_ready, g - 1)
                    dve.wait_ge(alibi_ready, g + 1)
                    wait_apart(dve, scores_ready, g + 1, passed)
                    for tt in range(TT):
                        last = dve.tensor_tensor_reduce(neg_scores[h % 2][:, tt, :], ps_scores[h % 2][:, tt, :],
                                                        alibi[h % 2][:, P - P * tt:P - P * tt + T], -Q_SCALE, 3e38,
                                                        ALU.add, ALU.min, neg_max[par][:, h, tt:tt + 1])
                    last.then_inc(max_ready, 1)

                def keep_probs_t(k, par, h):
                    g = head(k, par, h)
                    dve.wait_ge(probs_t_ready, g + 1)
                    if not is_first(k, par, h):
                        dve.wait_ge(pv_ready, g - 1)
                    dve.tensor_copy(probs_t[h % 2][:], ps_probs_t[h % 2][:]).then_inc(probs_t_kept[h % 2], 1)

                def keep_o(k, par):
                    b = batch(k, par)
                    dve.wait_ge(pv_ready, b * H + H)
                    dve.reciprocal(inv_sum[:], row_sum[par][:]).then_inc(inv_ready, 1)
                    dve.wait_ge(inv_ready, b + 1)
                    for tt in range(TT):
                        dve.tensor_tensor(o_norm[:, tt, :].rearrange("p (h d) -> p h d", d=DH),
                                          ps_o[:, tt, :].rearrange("p (h d) -> p h d", d=DH),
                                          inv_sum[:, tt, :].unsqueeze(2).to_broadcast([P, H, DH]),
                                          ALU.mult).then_inc(o_kept, 1)

                def add_attention(k, par, tt):
                    b = batch(k, par)
                    dve.wait_ge(wo_done, b * TT + (tt + 1))
                    dve.wait_ge(bias_added, b * TT + TT)
                    dve.tensor_tensor(x_mid[par][:, tt, :], ps_proj[:, tt, :], x_mid[par][:, tt, :],
                                      ALU.add).then_inc(x1_ready, 1)

                def x1_statistics(k, par):
                    b = batch(k, par)
                    dve.wait_ge(x1_ready, b * TT + TT)
                    for tt in range(TT):
                        dve.bn_stats(all_stats[:, ds(b * TT + tt, 1), :].rearrange("p o s -> p (o s)"),
                                     x_mid[par][:, tt, :]).then_inc(x1_stats, 1)

                def step(k, par, has_before, has_after):
                    prev, nxt = before(k, par), after(k, par)
                    for h in range(H):
                        if h == 0 and has_before and H - 1 in VECTOR_HEADS:
                            keep_probs_t(*prev, H - 1)
                        if h and h - 1 in VECTOR_HEADS:
                            keep_probs_t(k, par, h - 1)
                        if h + 1 < H:
                            score_max(k, par, h + 1)
                        elif has_after:
                            score_max(*nxt, 0)
                        if h + 2 < H:
                            head_alibi(k, par, h + 2)
                        elif has_after:
                            head_alibi(*nxt, h + 2 - H)
                        if has_before and h == 0:
                            keep_o(*prev)
                        if has_before and h == 1:
                            keep_t_lo(*prev, o_t, ot_kept)
                        if has_before and h in (O_SLOTS[1], O_SLOTS[3]):
                            add_attention(*prev, O_SLOTS.index(h) // 2)
                        if has_before and h == O_SLOTS[3] + 1:
                            x1_statistics(*prev)
                        if has_after:
                            if h == 0:
                                token_stats(*nxt)
                                token_moments(*nxt)
                            if h in (2, 3):
                                normalise(*nxt, h - 2)
                            if h == O_SLOTS[-1]:
                                keep_t_lo(*nxt, xn_t, xt_kept)
                            for half in range(2):
                                if h == Q_SLOTS[2 * half + 1]:
                                    keep_q_lo(*nxt, half)
                                if h == K_SLOTS[2 * half + 1]:
                                    keep_k_lo(*nxt, half)
                                if h == V_SLOTS[2 * half + 1]:
                                    keep_v(*nxt, half)

                token_stats(0, 0)
                token_moments(0, 0)
                for tt in range(TT):
                    normalise(0, 0, tt)
                halves = [(w, half) for w in (wq, wk, wv, wo) for half in range(2)]
                for n, (w, half) in enumerate(halves):
                    if n == 2:
                        keep_t_lo(0, 0, xn_t, xt_kept)
                    dve.wait_ge(w_hi_ready, n + 1)
                    dve.tensor_tensor(w[1][:, 2 * half:2 * half + 2, :], w_in[n % WEIGHT_BUFS][:],
                                      w[0][:, 2 * half:2 * half + 2, :], ALU.subtract).then_inc(w_ready, 1)
                dve.wait_ge(consts, 3)
                dve.wait_ge(small_load, 16 * 7)
                dve.tensor_copy(dist[:], dist_i[:]).then_inc(alibi_step, 1)
                dve.wait_ge(alibi_step, 1)
                dve.tensor_scalar(dist_neg[:], dist[:], -1.0, None, ALU.mult).then_inc(alibi_step, 1)
                dve.wait_ge(alibi_step, 2)
                dve.tensor_tensor(dist_neg[:], dist_neg[:], dist[:], ALU.min).then_inc(alibi_step, 1)
                dve.tensor_scalar(slope_scaled[:], slope_row[:], 1 / Q_SCALE, None, ALU.mult).then_inc(alibi_step, 1)
                dve.tensor_tensor(kernel_row[:, P:P + 1], kernel_row[:, P:P + 1], d_col[:],
                                  ALU.add).then_inc(kernel_ready, 2)
                for half in range(2):
                    keep_q_lo(0, 0, half)
                for half in range(2):
                    keep_k_lo(0, 0, half)
                for tt in range(TT):
                    keep_v(0, 0, tt)
                dve.wait_ge(alibi_step, 4)
                head_alibi(0, 0, 0)
                head_alibi(0, 0, 1)
                score_max(0, 0, 0)
                steps(dve, step)
                last = (B // 2 - 1, 1)
                if H - 1 in VECTOR_HEADS:
                    keep_probs_t(*last, H - 1)
                keep_o(*last)
                keep_t_lo(*last, o_t, ot_kept)
                for tt in range(TT):
                    add_attention(*last, tt)
                x1_statistics(*last)

            @block.scalar
            def _(act):
                def keep_t_hi(k, par, to, done, kept):
                    for half in range(2):
                        act.wait_ge(done, batch(k, par) * 2 + (half + 1))
                        if half:
                            act.wait_ge(kept, batch(k, par) * 4 + 2)
                        act.activation(to[0][:, 2 * half:2 * half + 2, :], ps_proj[:, half, :], ACT.Copy)\
                            .then_inc(kept, 1)

                def keep_q_hi(k, par, half):
                    act.wait_ge(q_done, batch(k, par) * 2 + (half + 1))
                    if half == 0 and not is_first(k, par):
                        for r in range(HPC):
                            act.wait_ge(stack_load[r], batch(k, par) * STACK_LOADS)
                    if half:
                        act.wait_ge(q_kept, batch(k, par) * (2 * EC) + 4)
                    for c in range(2):
                        f = 2 * half + c
                        act.activation(q_hi[:, f, :], ps_proj[:, half, c * T:c * T + T], ACT.Identity,
                                       bias=bq_col[:, f:f + 1]).then_inc(q_kept, 1)

                def keep_k_hi(k, par, half):
                    act.wait_ge(k_done, batch(k, par) * 2 + (half + 1))
                    if half == 0 and not is_first(k, par):
                        for r in range(HPC):
                            act.wait_ge(stack_load[r], batch(k, par) * STACK_LOADS)
                    if half:
                        act.wait_ge(k_kept, batch(k, par) * (2 * EC) + 4)
                    for c in range(2):
                        f = 2 * half + c
                        act.activation(k_hi[:, f, :], ps_proj[:, half, c * T:c * T + T], ACT.Identity,
                                       bias=bk_col[:, f:f + 1]).then_inc(k_kept, 1)

                def exponentials(k, par, h):
                    g = head(k, par, h)
                    act.wait_ge(max_ready, g + 1)
                    if not is_first(k, par, h):
                        act.wait_ge(probs_t_ready, g - 1)
                    for tt in range(TT):
                        last = act.activation(probs[h % 2][:, tt, :], neg_scores[h % 2][:, tt, :], ACT.Exp,
                                              bias=neg_max[par][:, h, tt:tt + 1], scale=-1.0,
                                              accum_out=row_sum[par][:, tt, HEADS[h]:HEADS[h] + 1])
                    last.then_inc(probs_ready, 1)

                def keep_probs_t(k, par, h):
                    g = head(k, par, h)
                    act.wait_ge(probs_t_ready, g + 1)
                    if not is_first(k, par, h):
                        act.wait_ge(pv_ready, g - 1)
                    act.activation(probs_t[h % 2][:], ps_probs_t[h % 2][:], ACT.Copy).then_inc(probs_t_kept[h % 2], 1)

                def step(k, par, has_before, has_after):
                    prev, nxt = before(k, par), after(k, par)
                    for h in range(H):
                        if h == 0 and has_before and H - 1 not in VECTOR_HEADS:
                            keep_probs_t(*prev, H - 1)
                        if h and h - 1 not in VECTOR_HEADS:
                            keep_probs_t(k, par, h - 1)
                        if has_before and h == 1:
                            keep_t_hi(*prev, o_t, ot_done, ot_kept)
                        if h + 1 < H:
                            exponentials(k, par, h + 1)
                        elif has_after:
                            exponentials(*nxt, 0)
                        if has_after and h == O_SLOTS[-1]:
                            keep_t_hi(*nxt, xn_t, xt_done, xt_kept)
                        for half in range(2):
                            if has_after and h == Q_SLOTS[2 * half + 1]:
                                keep_q_hi(*nxt, half)
                            if has_after and h == K_SLOTS[2 * half + 1]:
                                keep_k_hi(*nxt, half)

                halves = [(w, half) for w in (wq, wk, wv, wo) for half in range(2)]
                for n, (w, half) in enumerate(halves):
                    if n == 2:
                        keep_t_hi(0, 0, xn_t, xt_done, xt_kept)
                    act.wait_ge(w_load[n % WEIGHT_BUFS], n // WEIGHT_BUFS * 16 + 16)
                    act.activation(w[0][:, 2 * half:2 * half + 2, :], w_in[n % WEIGHT_BUFS][:], ACT.Copy)\
                        .then_inc(w_hi_ready, 1)
                act.wait_ge(small_load, 16 * 7)
                for half in range(2):
                    keep_q_hi(0, 0, half)
                for half in range(2):
                    keep_k_hi(0, 0, half)
                exponentials(0, 0, 0)
                steps(act, step)
                if H - 1 not in VECTOR_HEADS:
                    keep_probs_t(B // 2 - 1, 1, H - 1)
                keep_t_hi(B // 2 - 1, 1, o_t, ot_done, ot_kept)


        GB = B // 2
        GT = GB * TT
        PAIRS = SD * (SD + 1) // 2
        TAP_BUFS = 4
        FOLD = 2

        def pair_segments():
            segments = [(0, 0, 0, SD)]
            for d in range(1, SD // 2):
                segments += [(d * SD, 0, d, SD - d), (d * SD + SD - d, SD - d, 0, d)]
            return segments + [(SD // 2 * SD, 0, SD // 2, SD // 2)]

        with ExitStack() as scope:
            def sb(name, shape, dt=F32):
                return sbuf(name, shape, dt, scope)

            x_res = sbuf("x_res", [P, NT, E])
            ctx_g = sb("ctx_g", [P, EC, GB * T])
            q_g = sb("q_g", [P, EC, GB * T])
            taps = [sb(f"taps{i}", [P, E]) for i in range(TAP_BUFS)]
            pairs = [sb(f"pairs{i}", [P, EC, GB, PAIRS]) for i in range(2)]
            prods = [sb(f"prods{i}", [P, EC, GB, SD, SD]) for i in range(2)]
            xn_g = [sb(f"xn_g{i}", [P, TT, E]) for i in range(2)]
            ps_y = [psum(f"ps_y{i}", [P, EC, E], scope) for i in range(2)]

            x1_load = [sem(f"x1_load{g}") for g in range(2)]
            ctx_load = sem("ctx_load")
            tap_load = [sem(f"tap_load{i}") for i in range(TAP_BUFS)]
            c_rstd_step = sem("c_rstd_step")
            c_rstd = sem("c_rstd")
            c_xn = sem("c_xn")
            c_xt_done = sem("c_xt_done")
            c_xt_kept = sem("c_xt_kept")
            pairs_ready = sem("pairs_ready")
            y_ready = sem("y_ready")
            prods_ready = sem("prods_ready")
            folded = sem("folded")
            z_ready = sem("z_ready")
            zt_done = sem("zt_done")
            x1_moments = sem("x1_moments")
            x2_ready = sem("x2_ready")
            x2_stats = sem("x2_stats")
            x2_moments = sem("x2_moments")
            Y_START, PRODS_START, XT_START, X2_START = TAP_BUFS, 2, 2, 8
            Z_START, XT_DONE_START = 2, 2

            def by_head(tile):
                return tile[:, :, :].rearrange("p m (b s i) -> p m b s i", b=GB, s=SH)

            def head_of(tile, h, i, n):
                v = by_head(tile)[:, :, :, ds(h, 1), i:i + n]
                return v.rearrange("p m b s i -> p m b (s i)")

            skewed = bass.AP(tensor=kernel_pad, offset=1, ap=[[P + E, SH], [1, P], [1, E]])
            ctx_view = ctx_t.rearrange("(m p) n -> p m n", p=P)

            block = scope.enter_context(nc.Block())

            @block.sync
            def _(sp):
                sp.dma_start(x_res[:, 0:GT, :], x1_tiles[:, 0:GT, :]).then_inc(x1_load[0], 16)
                for g in range(2):
                    if g:
                        sp.wait_ge(pairs_ready, SH)
                    sp.dma_start(ctx_g[:], ctx_view[:, :, g * GB * T:(g + 1) * GB * T]).then_inc(ctx_load, 16)
                    with sp.Fori(0, SH // TAP_BUFS) as k:
                        for r in range(TAP_BUFS):
                            sp.wait_ge(y_ready, k * TAP_BUFS + (g * SH + r + 1 - TAP_BUFS + Y_START))
                            sp.dma_start(taps[r][:], skewed[ds(k * TAP_BUFS + r, 1), :, :].rearrange("o p c -> p (o c)"))\
                                .then_inc(tap_load[r], 16)

            @block.gpsimd
            def _(pool):
                pool.wait_ge(x1_moments, NT)
                reciprocal_sqrt(pool, all_rstd[:], all_moments[:, :, 1], var_eps[:], newton[:], c_rstd_step, 0, c_rstd, passed)

                def form_pairs(g, k, par):
                    pool.wait_ge(y_ready, k * 2 + (g * SH + par + 1 - 2 + Y_START))
                    for col, i, j, n in pair_segments():
                        last = pool.tensor_tensor(pairs[par][:, :, :, col:col + n],
                                                  head_of(ctx_g, k * 2 + par, i, n),
                                                  head_of(ctx_g, k * 2 + par, j, n), ALU.mult)
                    last.then_inc(pairs_ready, 1)

                def fold(g, k, par):
                    wait_apart(pool, prods_ready, k * 2 + (g * SH + par + 1 + PRODS_START), passed)
                    first = prods[par][:, :, :, :, 0:FOLD]
                    pool.tensor_tensor(first, first, prods[par][:, :, :, :, SD - FOLD:SD], ALU.add).then_inc(folded, 1)

                for g in range(2):
                    pool.wait_ge(ctx_load, 16 * g + 16)
                    for par in range(2):
                        form_pairs(g, 0, par)
                    with pool.Fori(1, SH // 2) as k:
                        for par in range(2):
                            form_pairs(g, k, par)
                            fold(g, k - 1, par)
                    for par in range(2):
                        fold(g, SH // 2 - 1, par)

            @block.tensor
            def _(pe):
                pe.sem_inc(y_ready, Y_START)
                pe.sem_inc(c_xt_done, XT_DONE_START)

                def x_transposes(g, k, par):
                    n = k * 2 + (par + g * GB)
                    pe.wait_ge(c_xn, n * TT + TT)
                    pe.wait_ge(c_xt_kept, n + (1 - 2 + XT_START))
                    for c in range(EC):
                        for tt in range(TT):
                            last = pe.transpose(ps_y[par][:, c, tt * P:tt * P + P], xn_g[par][:, tt, c * P:c * P + P],
                                                ident[:])
                    last.then_inc(c_xt_done, 1)

                def convolve(g, k, r):
                    h = k * TAP_BUFS + (r + g * SH)
                    par = r % 2
                    pe.wait_ge(pairs_ready, h + 1)
                    pe.wait_ge(tap_load[r], k * 16 + (g * (SH // TAP_BUFS) * 16 + 16))
                    pe.wait_ge(prods_ready, h + (1 - 2 + PRODS_START))
                    for lc in range(EC):
                        for mc in range(lc + 1):
                            block_cols = (lc - mc) * P
                            last = pe.matmul(ps_y[par][:, lc, 0:GB * PAIRS], taps[r][:, block_cols:block_cols + P],
                                             pairs[par][:, mc, :, :], start=(mc == 0), stop=(mc == lc))
                    last.then_inc(y_ready, 1)

                for g in range(2):
                    if g:
                        pe.wait_ge(x2_ready, GT + X2_START)
                    with pe.Fori(0, GB // 2) as k:
                        for par in range(2):
                            x_transposes(g, k, par)
                    pe.wait_ge(c_xt_kept, (g + 1) * GB + XT_START)
                    with pe.Fori(0, SH // TAP_BUFS) as k:
                        for r in range(TAP_BUFS):
                            convolve(g, k, r)
                    pe.wait_ge(z_ready, (g + 1) * SH + Z_START)
                    for t in range(GT):
                        bank = ps_y[t % 8 // EC][:, t % EC, :]
                        pe.wait_ge(x2_ready, g * GT + t + 1 - 8 + X2_START)
                        for c in range(EC):
                            last = pe.transpose(bank[:, c * P:c * P + P], q_g[:, c, t * P:t * P + P], ident[:])
                        last.then_inc(zt_done, 1)

            @block.scalar
            def _(act):
                act.sem_inc(c_xt_kept, XT_START)
                for g in range(2):
                    with act.Fori(0, GB // 2) as k:
                        for par in range(2):
                            n = k * 2 + (par + g * GB)
                            act.wait_ge(c_xt_done, n + 1 + XT_DONE_START)
                            if g:
                                act.wait_ge(zt_done, GT)
                            act.activation(q_g[:, :, ds(k * (2 * T) + par * T, T)], ps_y[par][:, :, 0:T], ACT.Copy)\
                                .then_inc(c_xt_kept, 1)
                    if g == 0:
                        act.dma_start(x_res[:, GT:NT, :], x1_tiles[:, GT:NT, :]).then_inc(x1_load[1], 16)

            @block.vector
            def _(dve):
                dve.sem_inc(prods_ready, PRODS_START)
                dve.sem_inc(x2_ready, X2_START)
                dve.sem_inc(z_ready, Z_START)

                def row(tile, t):
                    return tile[:, ds(t, 1), :].rearrange("p o e -> p (o e)")

                def normalise(g, k, par):
                    n = k * 2 + (par + g * GB)
                    dve.wait_ge(c_xt_done, n + (1 - 2 + XT_DONE_START))
                    for tt in range(TT):
                        t = n * TT + tt
                        dve.tensor_scalar(xn_g[par][:, tt, :], row(x_res, t), all_moments[:, ds(t, 1), 0], all_rstd[:, ds(t, 1)],
                                          ALU.subtract, ALU.mult).then_inc(c_xn, 1)

                def multiply(g, k, par):
                    h, own = k * 2 + (par + g * SH), k * 2 + par
                    dve.wait_ge(y_ready, h + (1 + Y_START))
                    dve.wait_ge(z_ready, h + (1 - 2 + Z_START))
                    y = ps_y[par][:, :, 0:GB * PAIRS].rearrange("p c (b q) -> p c b q", b=GB)
                    for col, i, j, n in pair_segments():
                        d = col // SD
                        uses = [(i, j, d)]
                        if d == SD // 2:
                            uses += [(j, i, d)]
                        elif d:
                            uses += [(j, i, SD // 2 + d)]
                        for to, q_from, term in uses:
                            last = dve.tensor_tensor(prods[par][:, :, :, to:to + n, term], y[:, :, :, col:col + n],
                                                     head_of(q_g, own, q_from, n), ALU.mult)
                    last.then_inc(prods_ready, 1)

                def add_up(g, k, par):
                    wait_apart(dve, folded, k * 2 + (par + g * SH + 1), passed)
                    dve.tensor_reduce(head_of(q_g, k * 2 + par, 0, SD), prods[par][:, :, :, :, 0:SD - FOLD], AX_X,
                                      ALU.add).then_inc(z_ready, 1)

                for t in range(NT):
                    dve.bn_aggr(all_moments[:, t, :], all_stats[:, t, :]).then_inc(x1_moments, 1)
                dve.wait_ge(c_rstd, 1)
                for g in range(2):
                    dve.wait_ge(x1_load[g], 16)
                    with dve.Fori(0, GB // 2) as k:
                        for par in range(2):
                            normalise(g, k, par)
                    dve.wait_ge(c_xt_kept, (g + 1) * GB + XT_START)
                    multiply(g, 0, 0)
                    multiply(g, 0, 1)
                    add_up(g, 0, 0)
                    with dve.Fori(1, SH // 2) as k:
                        multiply(g, k, 0)
                        add_up(g, k - 1, 1)
                        multiply(g, k, 1)
                        add_up(g, k, 0)
                    add_up(g, SH // 2 - 1, 1)
                    for t in range(GT + 2):
                        n = g * GT + t
                        if t < GT:
                            dve.wait_ge(zt_done, n + 1)
                            dve.tensor_tensor(x_res[:, n, :], ps_y[t % 8 // EC][:, t % EC, :], x_res[:, n, :],
                                              ALU.add).then_inc(x2_ready, 1)
                        if 1 <= t <= GT:
                            dve.wait_ge(x2_ready, n + X2_START)
                            dve.bn_stats(all_stats[:, n - 1, :], x_res[:, n - 1, :]).then_inc(x2_stats, 1)
                        if t >= 2:
                            dve.wait_ge(x2_stats, n - 1)
                            dve.bn_aggr(all_moments[:, n - 2, :], all_stats[:, n - 2, :]).then_inc(x2_moments, 1)


        BATCH = 8
        N_BATCHES = NT // BATCH
        ROUNDS = N_BATCHES // 2
        RING = 8
        BUFS = 4
        AHEAD = 3
        FC = FI // P
        ROUTE_OPS = 24
        assert NE == 8 and N_TILES % RING == 0 and N_BATCHES % 2 == 0 and ROUNDS >= 2 and RING == 2 * BUFS

        with ExitStack() as scope:
            def sb(name, shape, dt=F32):
                return sbuf(name, shape, dt, scope)

            w_gu = sb("w_gu", [P, NE, EC, 2 * FI])
            w_down = sb("w_down", [P, NE, FC, E])
            w_router = sb("w_router", [P, EC, NE])
            tile_expert_i = sb("tile_expert_i", [P, N_TILES], I32)
            tile_row_i = sb("tile_row_i", [P, N_TILES], I32)

            def sb_in(part, name, shape, dt=F32):
                return sbuf(name, shape, dt, part)

            with ExitStack() as routing:
                xn_c = [sb_in(routing, f"xn_c{i}", [P, E]) for i in range(BATCH)]
                xt_c = [sb_in(routing, f"xt_c{i}", [P, EC, P]) for i in range(2)]
                backward_i = sb_in(routing, "backward_i", [P, NE], I32)
                backward = sb_in(routing, "backward", [P, NE])
                first_row_i = sb_in(routing, "first_row_i", [P, NE], I32)
                first_row = sb_in(routing, "first_row", [P, NE])
                pair_i = sb_in(routing, "pair_i", [P, NT, TOP, 2], I32)
                pair = sb_in(routing, "pair", [P, NT, TOP, 2])
                ones_b = sb_in(routing, "ones_b", [P, P], BF16)
                before_b = sb_in(routing, "before_b", [P, P], BF16)
                best = [sb_in(routing, f"best{i}", [P, BATCH]) for i in range(TOP)]
                is_best = sb_in(routing, "is_best", [P, BATCH, NE])
                rest = sb_in(routing, "rest", [P, BATCH, NE])
                which = sb_in(routing, "which", [P, BATCH])
                one_hot = sb_in(routing, "one_hot", [P, BATCH, TOP, NE])
                chosen_b = sb_in(routing, "chosen_b", [P, BATCH, NE], BF16)
                ratio = [sb_in(routing, f"ratio{i}", [P, BATCH]) for i in range(2)]
                ratio_sum = sb_in(routing, "ratio_sum", [P, BATCH])
                place = sb_in(routing, "place", [P, BATCH, NE])
                place_of = sb_in(routing, "place_of", [P, BATCH, TOP, NE])
                position = sb_in(routing, "position", [P, BATCH, TOP])
                batch_sum = sb_in(routing, "batch_sum", [P, NE])
                lane_sum = sb_in(routing, "lane_sum", [P, NE])
                lane_sum_b = sb_in(routing, "lane_sum_b", [P, NE], BF16)
                pair_rows = [sb_in(routing, f"pair_rows{i}", [P, BATCH, TOP, PAIR_ROW]) for i in range(2)]
                dest = [sb_in(routing, f"dest{i}", [P, BATCH, TOP], U32) for i in range(2)]
                tiles_i = sb_in(routing, "tiles_i", [P, NE], I32)
                tiles_f = sb_in(routing, "tiles_f", [P, NE])
                tile_end = sb_in(routing, "tile_end", [P, NE])
                ones_f = sb_in(routing, "ones_f", [P, NE])
                tile_iota_i = sb_in(routing, "tile_iota_i", [P, N_TILES], I32)
                tile_iota = sb_in(routing, "tile_iota", [P, N_TILES])
                tile_past = sb_in(routing, "tile_past", [P, N_TILES, NE])
                tile_expert = sb_in(routing, "tile_expert", [P, N_TILES])
                tile_start = sb_in(routing, "tile_start", [P, N_TILES])
            with ExitStack() as tiling:
                pair_row = [sb_in(tiling, f"pair_row{i}", [P, PAIR_ROW]) for i in range(RING)]
                take = [sb_in(tiling, f"take{i}", [P, 1], U32) for i in range(RING)]
                back = [sb_in(tiling, f"back{i}", [P, 1], U32) for i in range(RING)]
                srow = [sb_in(tiling, f"srow{i}", [P, E]) for i in range(BUFS)]
                st = [sb_in(tiling, f"st{i}", [P, EC, P]) for i in range(2)]
                silu_g = [sb_in(tiling, f"silu_g{i}", [P, FI]) for i in range(2)]
                hidden = [sb_in(tiling, f"hidden{i}", [P, FI]) for i in range(2)]
                hidden_t = [sb_in(tiling, f"hidden_t{i}", [P, FC, P]) for i in range(2)]
                y_row = [sb_in(tiling, f"y_row{i}", [P, E]) for i in range(BUFS)]

            ps_x = psum("ps_x", [P, 2, E], scope)
            ps_gu = psum("ps_gu", [P, 2, 2 * FI], scope)
            ps_ht = psum("ps_ht", [P, E], scope)
            ps_down = psum("ps_down", [P, 2, E], scope)
            ps_count = psum("ps_count", [P, E], scope)
            ps_logit = [ps_gu[:, i, :] for i in range(2)]
            ps_rank = ps_ht

            router_load = sem("router_load")
            w_load = sem("w_load")
            m_consts = sem("m_consts")
            m_rstd_step = sem("m_rstd_step")
            m_rstd = sem("m_rstd")
            n_ready = sem("n_ready")
            n_stored = [sem(f"n_stored{i}") for i in range(BATCH)]
            nt_done = sem("nt_done")
            nt_kept = sem("nt_kept")
            logits_done = sem("logits_done")
            logits_read = sem("logits_read")
            const_step = sem("const_step")
            route = sem("route")
            gap_ready = sem("gap_ready")
            ratio_ready = sem("ratio_ready")
            chosen_ready = sem("chosen_ready")
            ranked = sem("ranked")
            pair_rows_ready = sem("pair_rows_ready")
            pairs_scattered = [sem(f"pairs_scattered{i}") for i in range(2)]
            summed = sem("summed")
            counted = sem("counted")
            list_step = sem("list_step")
            tiles_known = sem("tiles_known")
            pair_load = [sem(f"pair_load{i}") for i in range(RING)]
            take_ready = sem("take_ready")
            row_load = [sem(f"row_load{i}") for i in range(BUFS)]
            st_done = sem("st_done")
            st_kept = sem("st_kept")
            gu_done = sem("gu_done")
            silu_ready = sem("silu_ready")
            hidden_ready = sem("hidden_ready")
            ht_done = sem("ht_done")
            ht_kept = sem("ht_kept")
            down_done = sem("down_done")
            y_ready = sem("y_row_ready")
            y_scattered = [sem(f"y_scattered{i}") for i in range(BUFS)]
            y_load = [sem(f"y_load{i}") for i in range(8)]
            y_added = sem("y_added")
            store = sem("store")
            NT_START, HIDDEN_START, DOWN_START, Y_START, KEPT_START = 2, 2, 2, 2, 1

            y_view = expert_out.rearrange("(s t p) e -> p s t e", s=TOP, p=P)
            xn_view = xn_rows.rearrange("(t p) e -> p t e", p=P)
            PAIR = 2
            Y_BUFS = 8
            N_PAIRS = NT // PAIR
            y_in = [w_gu[:, i, :, :].rearrange("p (s t) e -> p s t e", s=TOP) for i in range(Y_BUFS)]

            def row(tile, t):
                return tile[:, ds(t, 1), :].rearrange("p o e -> p (o e)")

            def first_round(k):
                return isinstance(k, int) and k == 0

            def rounds(eng, n, per_round, emit):
                for k in (0, None, n - 1):
                    if k is None and n == 2:
                        pass
                    elif k is None:
                        with eng.Fori(1, n - 1) as k:
                            for r in range(per_round):
                                emit(k, r, False)
                    else:
                        for r in range(per_round):
                            emit(k, r, k == n - 1)

            def route_steps(eng, emit):
                rounds(eng, ROUNDS, 2, lambda k, par, last: emit(k, par, last and par == 1))

            def batch_after(k, par):
                return (k, 1) if par == 0 else (k + 1, 0)

            def batch_before(k, par):
                return (k, 0) if par == 1 else (k - 1, 1)

            def batch_no(k, par):
                return k * 2 + par

            def tile_steps(eng, emit):
                rounds(eng, N_TILES // RING, RING, emit)

            def at(kk, r, ahead=0):
                return (kk + 1, r + ahead - RING) if r + ahead >= RING else (kk, r + ahead)

            def exists(last, r, ahead):
                return not (last and r + ahead >= RING)

            def tile_no(kk, r):
                return kk * RING + r

            def turn(kk, r):
                return kk * (RING // BUFS) + r // BUFS

            block = scope.enter_context(nc.Block())

            @block.sync
            def _(sp):
                sp.dma_start(w_router[:], router_t.rearrange("(c p) n -> p c n", p=P)).then_inc(router_load, 16)
                for e in range(NE):
                    sp.wait_ge(n_ready, e * (NT // NE) + 1)
                    sp.dma_start(w_gu[:, e, :, :], gate_up[e].rearrange("(c p) g f -> p c (g f)", p=P)).then_inc(w_load, 16)
                    sp.dma_start(w_down[:, e, :, :], down[e].rearrange("(c p) n -> p c n", p=P)).then_inc(w_load, 16)
                sp.wait_ge(tiles_known, 1)
                for par in range(2):
                    sp.wait_ge(pairs_scattered[par], ROUNDS * BATCH * TOP * 16)
                for i in range(BATCH):
                    sp.wait_ge(n_stored[i], N_BATCHES * 16)

                def load_pairs(kk, r, last):
                    n = tile_no(kk, r)
                    if not first_round(kk):
                        wait_apart(sp, y_ready, n + 1 - RING + Y_START, passed)
                        wait_apart(sp, pair_load[r], kk * 16, passed)
                    first = sp.value_load(tile_row_i[0:1, ds(n, 1)], min_val=0, max_val=TABLE_ROWS - P)
                    sp.dma_start(pair_row[r][:], row_table[ds(first, P), :]).then_inc(pair_load[r], 16)

                tile_steps(sp, load_pairs)
                for i in range(BUFS):
                    sp.wait_ge(y_scattered[i], N_TILES // BUFS * 16)
                for t in range(N_PAIRS):
                    if t >= Y_BUFS:
                        sp.wait_ge(y_added, (t - Y_BUFS) * TOP + TOP)
                        sp.wait_ge(y_load[t % Y_BUFS], t // Y_BUFS * TOP * 16)
                    for s in range(TOP):
                        sp.dma_start(y_in[t % Y_BUFS][:, s, :, :], y_view[:, s, t * PAIR:t * PAIR + PAIR, :])\
                          .then_inc(y_load[t % Y_BUFS], 16)

            @block.gpsimd
            def _(pool):
                reciprocal_sqrt(pool, all_rstd[:], all_moments[:, :, 1], var_eps[:], newton[:], m_rstd_step, 0, m_rstd,
                                passed)
                pool.iota(backward_i[:], pattern=[[-1, NE]], base=NE, channel_multiplier=0).then_inc(m_consts, 1)
                pool.iota(first_row_i[:], pattern=[[N_TOK, NE]], base=0, channel_multiplier=0).then_inc(m_consts, 1)
                for s in range(TOP):
                    pool.iota(pair_i[:, :, s, TOKEN], pattern=[[P, NT]], base=0, channel_multiplier=1).then_inc(m_consts, 1)
                    pool.iota(pair_i[:, :, s, BACK], pattern=[[P, NT]], base=s * N_TOK, channel_multiplier=1)\
                        .then_inc(m_consts, 1)
                pool.iota(tile_iota_i[:], pattern=[[1, N_TILES]], base=0, channel_multiplier=0).then_inc(m_consts, 1)
                pool.memset(ones_b[:], 1.0).then_inc(m_consts, 1)
                pool.memset(ones_f[:], 1.0).then_inc(m_consts, 1)
                pool.memset(lane_sum[:], 0.0).then_inc(m_consts, 1)
                pool.memset(lane_sum_b[:], 0.0).then_inc(m_consts, 1)
                for par in range(2):
                    pool.memset(pair_rows[par][:], 0.0).then_inc(m_consts, 1)
                pool.wait_ge(m_consts, 13)
                pool.affine_select(out=before_b[:], in_=ones_b[:], compare_op=ALU.is_gt, fill=0.0, base=0,
                                   pattern=[[1, P]], channel_multiplier=-1).then_inc(m_consts, 1)

                def scatter_pairs(k, par, last):
                    wait_apart(pool, pair_rows_ready, batch_no(k, par) + 1, passed)
                    for i in range(BATCH):
                        for s in range(TOP):
                            pool.indirect_dma_start(
                                out=row_table[:, :], out_offset=bass.IndirectOffsetOnAxis(ap=dest[par][:, i, s:s + 1], axis=0),
                                in_=pair_rows[par][:, i, s, :], in_offset=None, bounds_check=TABLE_ROWS - 1,
                                oob_is_err=False).then_inc(pairs_scattered[par], 16)

                with pool.Fori(0, ROUNDS) as k:
                    for par in range(2):
                        scatter_pairs(k, par, False)

                def gather(kk, r):
                    n = tile_no(kk, r)
                    wait_apart(pool, take_ready, n + 1, passed)
                    if not (first_round(kk) and r < BUFS):
                        wait_apart(pool, st_done, n + 1 - BUFS, passed)
                    pool.indirect_dma_start(
                        out=srow[r % BUFS][:], out_offset=None, in_=xn_rows[:, :],
                        in_offset=bass.IndirectOffsetOnAxis(ap=take[r][:, 0:1], axis=0), bounds_check=N_TOK - 1,
                        oob_is_err=False).then_inc(row_load[r % BUFS], 16)

                def tile_step(kk, r, last):
                    if exists(last, r, AHEAD):
                        gather(*at(kk, r, AHEAD))
                    wait_apart(pool, y_ready, tile_no(kk, r) + 1 + Y_START, passed)
                    pool.indirect_dma_start(
                        out=expert_out[:, :], out_offset=bass.IndirectOffsetOnAxis(ap=back[r][:, 0:1], axis=0),
                        in_=y_row[r % BUFS][:], in_offset=None, bounds_check=TOP * N_TOK - 1,
                        oob_is_err=False).then_inc(y_scattered[r % BUFS], 16)

                for i in range(BATCH):
                    pool.wait_ge(n_stored[i], N_BATCHES * 16)
                for r in range(AHEAD):
                    gather(0, r)
                tile_steps(pool, tile_step)

            @block.tensor
            def _(pe):
                pe.sem_inc(down_done, DOWN_START)

                def n_transposes(k, par, i):
                    t = batch_no(k, par) * BATCH + i
                    pe.wait_ge(n_ready, t + 1)
                    pe.wait_ge(nt_kept, t + 1 - 2 + NT_START)
                    for c in range(EC):
                        last = pe.transpose(ps_x[:, i % 2, c * P:c * P + P], xn_c[i][:, c * P:c * P + P], ident[:])
                    last.then_inc(nt_done, 1)

                def logits(k, par, i):
                    t = batch_no(k, par) * BATCH + i
                    pe.wait_ge(nt_kept, t + 1 + NT_START)
                    if i == 0 and not first_round(k):
                        pe.wait_ge(logits_read, batch_no(k, par) - 1)
                    for c in range(EC):
                        last = pe.matmul(ps_logit[par][:, i * NE:i * NE + NE], xt_c[i % 2][:, c, :], w_router[:, c, :],
                                         start=(c == 0), stop=(c == EC - 1))
                    if i == BATCH - 1:
                        last.then_inc(logits_done, 1)

                def rank(k, par):
                    pe.wait_ge(chosen_ready, batch_no(k, par) + 1)
                    cols = BATCH * NE
                    pe.matmul(ps_rank[:, 0:cols], before_b[:], chosen_b[:, :, :], start=True, stop=False)
                    for d in range(1, BATCH):
                        pe.matmul(ps_rank[:, d * NE:cols], ones_b[:], chosen_b[:, 0:BATCH - d, :], start=False, stop=False)
                    pe.matmul(ps_rank[:, 0:cols], ones_b[:], lane_sum_b[:].unsqueeze(1).to_broadcast([P, BATCH, NE]),
                              start=False, stop=True).then_inc(ranked, 1)

                def route_step(k, par, last):
                    for i in range(BATCH):
                        if i + 1 < BATCH:
                            n_transposes(k, par, i + 1)
                        elif not last:
                            n_transposes(*batch_after(k, par), 0)
                        logits(k, par, i)
                        if i == 1 and not (first_round(k) and par == 0):
                            rank(*batch_before(k, par))
                    if last:
                        rank(k, par)

                pe.wait_ge(router_load, 16)
                pe.wait_ge(m_consts, 14)
                n_transposes(0, 0, 0)
                route_steps(pe, route_step)
                pe.wait_ge(summed, N_BATCHES)
                pe.matmul(ps_count[:, 0:NE], ones_b[:], lane_sum_b[:], start=True, stop=True).then_inc(counted, 1)

                def s_transposes(kk, r):
                    n = tile_no(kk, r)
                    pe.wait_ge(row_load[r % BUFS], turn(kk, r) * 16 + 16)
                    pe.wait_ge(st_kept, n + KEPT_START)
                    for c in range(EC):
                        last = pe.transpose(ps_x[:, 0, c * P:c * P + P], srow[r % BUFS][:, c * P:c * P + P], ident[:])
                    last.then_inc(st_done, 1)

                def expert(kk, r):
                    return pe.value_load(tile_expert_i[0:1, ds(tile_no(kk, r), 1)], min_val=0, max_val=NE - 1)

                def gate_and_up(kk, r):
                    n, e = tile_no(kk, r), expert(kk, r)
                    pe.wait_ge(st_kept, n + 1 + KEPT_START)
                    pe.wait_ge(hidden_ready, n + 1 - 2 + HIDDEN_START)
                    for c in range(EC):
                        last = pe.matmul(ps_gu[:, r % 2, :], st[r % 2][:, c, :],
                                         w_gu[:, ds(e, 1), c, :].rearrange("p o f -> p (o f)"),
                                         start=(c == 0), stop=(c == EC - 1))
                    last.then_inc(gu_done, 1)

                def h_transposes(kk, r):
                    n = tile_no(kk, r)
                    pe.wait_ge(hidden_ready, n + 1 + HIDDEN_START)
                    pe.wait_ge(ht_kept, n + KEPT_START)
                    for c in range(FC):
                        last = pe.transpose(ps_ht[:, c * P:c * P + P], hidden[r % 2][:, c * P:c * P + P], ident[:])
                    last.then_inc(ht_done, 1)

                def down_rows(kk, r):
                    n, e = tile_no(kk, r), expert(kk, r)
                    pe.wait_ge(ht_kept, n + 1 + KEPT_START)
                    pe.wait_ge(y_ready, n + 1 - 2 + Y_START)
                    for c in range(FC):
                        last = pe.matmul(ps_down[:, r % 2, :], hidden_t[r % 2][:, c, :],
                                         w_down[:, ds(e, 1), c, :].rearrange("p o f -> p (o f)"),
                                         start=(c == 0), stop=(c == FC - 1))
                    last.then_inc(down_done, 1)

                def tile_step(kk, r, last):
                    if exists(last, r, 2):
                        s_transposes(*at(kk, r, 2))
                    h_transposes(kk, r)
                    if exists(last, r, 1):
                        gate_and_up(*at(kk, r, 1))
                    down_rows(kk, r)

                pe.wait_ge(w_load, 16 * 2 * NE)
                pe.wait_ge(tiles_known, 1)
                s_transposes(0, 0)
                s_transposes(0, 1)
                gate_and_up(0, 0)
                tile_steps(pe, tile_step)

            @block.scalar
            def _(act):
                act.sem_inc(nt_kept, NT_START)
                act.sem_inc(y_ready, Y_START)
                act.sem_inc(st_kept, KEPT_START)

                def score_ratio(k, par):
                    act.wait_ge(gap_ready, batch_no(k, par) + 1)
                    act.activation(ratio[par][:], ratio[par][:], ACT.Exp).then_inc(ratio_ready, 1)

                def route_step(k, par, last):
                    for i in range(BATCH):
                        t = batch_no(k, par) * BATCH + i
                        act.wait_ge(n_ready, t + 1)
                        if not (first_round(k) and par == 0):
                            act.wait_ge(n_stored[i], batch_no(k, par) * 16)
                        act.dma_start(xn_view[:, ds(t, 1), :], xn_c[i][:].unsqueeze(1)).then_inc(n_stored[i], 16)
                        act.wait_ge(nt_done, t + 1)
                        act.activation(xt_c[i % 2][:], ps_x[:, i % 2, :], ACT.Copy).then_inc(nt_kept, 1)
                        if i == 1 and not (first_round(k) and par == 0):
                            score_ratio(*batch_before(k, par))
                    if last:
                        score_ratio(k, par)

                route_steps(act, route_step)

                def keep_st(kk, r):
                    act.wait_ge(st_done, tile_no(kk, r) + 1)
                    act.activation(st[r % 2][:], ps_x[:, 0, :], ACT.Copy).then_inc(st_kept, 1)

                def silu_of(kk, r):
                    n = tile_no(kk, r)
                    act.wait_ge(gu_done, n + 1)
                    act.wait_ge(hidden_ready, n + 1 - 2 + HIDDEN_START)
                    act.activation(silu_g[r % 2][:], ps_gu[:, r % 2, 0:FI], ACT.Silu).then_inc(silu_ready, 1)

                def weigh(kk, r):
                    n = tile_no(kk, r)
                    act.wait_ge(down_done, n + 1 + DOWN_START)
                    if not (first_round(kk) and r < BUFS):
                        act.wait_ge(y_scattered[r % BUFS], turn(kk, r) * 16)
                    act.activation(y_row[r % BUFS][:], ps_down[:, r % 2, :], ACT.Copy,
                                   scale=pair_row[r][:, SCORE:SCORE + 1]).then_inc(y_ready, 1)

                def tile_step(kk, r, last):
                    if exists(last, r, 2):
                        keep_st(*at(kk, r, 2))
                    if exists(last, r, 1):
                        silu_of(*at(kk, r, 1))
                    weigh(kk, r)

                keep_st(0, 0)
                keep_st(0, 1)
                silu_of(0, 0)
                tile_steps(act, tile_step)
                for t in range(N_PAIRS):
                    act.wait_ge(y_added, t * TOP + TOP)
                    act.dma_start(out_tiles[:, t * PAIR:t * PAIR + PAIR, :], x_res[:, t * PAIR:t * PAIR + PAIR, :])\
                       .then_inc(store, 16)
                act.wait_ge(store, N_PAIRS * 16)

            @block.vector
            def _(dve):
                dve.sem_inc(hidden_ready, HIDDEN_START)
                dve.sem_inc(ht_kept, KEPT_START)

                def n_rows(k, par):
                    for i in range(BATCH):
                        t = batch_no(k, par) * BATCH + i
                        if not (first_round(k) and par == 0):
                            dve.wait_ge(nt_done, t + 1 - BATCH)
                            dve.wait_ge(n_stored[i], batch_no(k, par) * 16)
                        dve.tensor_scalar(xn_c[i][:], row(x_res, t), all_moments[:, ds(t, 1), 0], all_rstd[:, ds(t, 1)],
                                          ALU.subtract, ALU.mult).then_inc(n_ready, 1)

                def route_batch(k, par):
                    b = batch_no(k, par)
                    steps = [0]

                    def chain(instruction):
                        steps[0] += 1
                        instruction.then_inc(route, 1)
                        wait_apart(dve, route, b * ROUTE_OPS + steps[0], passed)

                    def by_token(tile):
                        return tile[:].unsqueeze(2).to_broadcast([P, BATCH, NE])

                    logit = ps_logit[par][:, 0:BATCH * NE].rearrange("p (t n) -> p t n", n=NE)
                    numbers = backward[:].unsqueeze(1).to_broadcast([P, BATCH, NE])
                    wait_apart(dve, logits_done, b + 1, passed)
                    for s, values in enumerate((logit, rest[:])):
                        chain(dve.tensor_reduce(best[s][:], values, AX_X, ALU.max))
                        chain(dve.tensor_tensor(is_best[:], values, by_token(best[s]), ALU.is_equal))
                        chain(dve.tensor_tensor(is_best[:], is_best[:], numbers, ALU.mult))
                        chain(dve.tensor_reduce(which[:], is_best[:], AX_X, ALU.max))
                        chain(dve.tensor_tensor(one_hot[:, :, s, :], numbers, by_token(which), ALU.is_equal))
                        if s == 0:
                            chain(dve.scalar_tensor_tensor(rest[:], one_hot[:, :, 0, :], -3.0e38, logit, ALU.mult, ALU.add))
                            dve.sem_inc(logits_read, 1)
                    dve.tensor_tensor(chosen_b[:], one_hot[:, :, 0, :], one_hot[:, :, 1, :], ALU.add).then_inc(chosen_ready, 1)
                    dve.tensor_tensor(ratio[par][:], best[1][:], best[0][:], ALU.subtract).then_inc(gap_ready, 1)
                    if not first_round(k):
                        wait_apart(dve, pairs_scattered[par], k * (BATCH * TOP * 16), passed)
                    chain(dve.tensor_copy(pair_rows[par][:, :, :, 0:2], pair[:, ds(b * BATCH, BATCH), :, :]))
                    wait_apart(dve, ratio_ready, b + 1, passed)
                    chain(dve.tensor_scalar(ratio_sum[:], ratio[par][:], 1.0, None, ALU.add))
                    chain(dve.reciprocal(pair_rows[par][:, :, 0, SCORE], ratio_sum[:]))
                    chain(dve.tensor_tensor(pair_rows[par][:, :, 1, SCORE], ratio[par][:], pair_rows[par][:, :, 0, SCORE],
                                            ALU.mult))
                    wait_apart(dve, ranked, b + 1, passed)
                    chain(dve.tensor_tensor(place[:], ps_rank[:, 0:BATCH * NE].rearrange("p (t n) -> p t n", n=NE),
                                            first_row[:].unsqueeze(1).to_broadcast([P, BATCH, NE]), ALU.add))
                    for s in range(TOP):
                        chain(dve.tensor_tensor(place_of[:, :, s, :], place[:], one_hot[:, :, s, :], ALU.mult))
                    chain(dve.tensor_reduce(position[:], place_of[:], AX_X, ALU.add))
                    chain(dve.tensor_copy(dest[par][:], position[:]))
                    dve.sem_inc(pair_rows_ready, 1)
                    chain(dve.tensor_reduce(batch_sum[:], chosen_b[:].rearrange("p t n -> p n t"), AX_X, ALU.add))
                    chain(dve.tensor_tensor(lane_sum[:], lane_sum[:], batch_sum[:], ALU.add))
                    chain(dve.tensor_copy(lane_sum_b[:], lane_sum[:]))
                    dve.sem_inc(summed, 1)
                    assert steps[0] <= ROUTE_OPS
                    dve.sem_inc(route, ROUTE_OPS - steps[0])

                def route_step(k, par, last):
                    if not last:
                        n_rows(*batch_after(k, par))
                    route_batch(k, par)

                dve.wait_ge(m_rstd, 1)
                n_rows(0, 0)
                dve.wait_ge(m_consts, 14)
                for n, (to, of) in enumerate(((backward, backward_i), (first_row, first_row_i), (pair, pair_i),
                                              (tile_iota, tile_iota_i))):
                    dve.tensor_copy(to[:], of[:]).then_inc(const_step, 1)
                dve.wait_ge(const_step, 4)
                route_steps(dve, route_step)

                step = [0]

                def chain(instruction):
                    step[0] += 1
                    instruction.then_inc(list_step, 1)
                    dve.wait_ge(list_step, step[0])

                dve.wait_ge(counted, 1)
                chain(dve.tensor_scalar(tiles_i[:], ps_count[:, 0:NE], float(P - 1), None, ALU.add))
                chain(dve.tensor_scalar(tiles_i[:], tiles_i[:], 7, None, ALU.arith_shift_right))
                chain(dve.tensor_copy(tiles_f[:], tiles_i[:]))
                chain(dve.tensor_tensor_scan(tile_end[:], ones_f[:], tiles_f[:], 0.0, ALU.mult, ALU.add))
                chain(dve.tensor_tensor(tile_past[:], tile_iota[:].unsqueeze(2).to_broadcast([P, N_TILES, NE]),
                                        tile_end[:].unsqueeze(1).to_broadcast([P, N_TILES, NE]), ALU.is_ge))
                chain(dve.tensor_reduce(tile_expert[:], tile_past[:], AX_X, ALU.add))
                chain(dve.tensor_tensor(tile_past[:], tile_past[:], tiles_f[:].unsqueeze(1).to_broadcast([P, N_TILES, NE]),
                                        ALU.mult))
                chain(dve.tensor_reduce(tile_start[:], tile_past[:], AX_X, ALU.add))
                chain(dve.tensor_tensor(tile_iota[:], tile_iota[:], tile_start[:], ALU.subtract))
                chain(dve.tensor_scalar(tile_iota[:], tile_iota[:], float(P), None, ALU.mult))
                chain(dve.scalar_tensor_tensor(tile_start[:], tile_expert[:], float(N_TOK), tile_iota[:], ALU.mult, ALU.add))
                chain(dve.tensor_copy(tile_row_i[:], tile_start[:]))
                chain(dve.tensor_scalar(tile_expert[:], tile_expert[:], float(NE - 1), None, ALU.min))
                dve.tensor_copy(tile_expert_i[:], tile_expert[:]).then_inc(tiles_known, 1)

                def read_pairs(kk, r):
                    n = tile_no(kk, r)
                    dve.wait_ge(pair_load[r], kk * 16 + 16)
                    if not first_round(kk):
                        dve.wait_ge(y_scattered[r % BUFS], turn(kk, r) * 16 - 16)
                    dve.tensor_copy(take[r][:], pair_row[r][:, TOKEN:TOKEN + 1])
                    dve.tensor_copy(back[r][:], pair_row[r][:, BACK:BACK + 1]).then_inc(take_ready, 1)

                def keep_ht(kk, r):
                    n = tile_no(kk, r)
                    dve.wait_ge(ht_done, n + 1)
                    dve.wait_ge(down_done, n + 1 - 2 + DOWN_START)
                    dve.tensor_copy(hidden_t[r % 2][:].rearrange("p c t -> p (c t)"), ps_ht[:, 0:FI]).then_inc(ht_kept, 1)

                def gated(kk, r):
                    dve.wait_ge(silu_ready, tile_no(kk, r) + 1)
                    dve.tensor_tensor(hidden[r % 2][:], ps_gu[:, r % 2, FI:2 * FI], silu_g[r % 2][:], ALU.mult)\
                       .then_inc(hidden_ready, 1)

                def tile_step(kk, r, last):
                    keep_ht(kk, r)
                    if exists(last, r, AHEAD + 1):
                        read_pairs(*at(kk, r, AHEAD + 1))
                    if exists(last, r, 1):
                        gated(*at(kk, r, 1))

                for r in range(AHEAD + 1):
                    read_pairs(0, r)
                gated(0, 0)
                tile_steps(dve, tile_step)
                for t in range(N_PAIRS):
                    tiles = x_res[:, t * PAIR:t * PAIR + PAIR, :]
                    dve.wait_ge(y_load[t % Y_BUFS], (t // Y_BUFS + 1) * TOP * 16)
                    for s in range(TOP):
                        if s:
                            dve.wait_ge(y_added, t * TOP + s)
                        dve.tensor_tensor(tiles, tiles, y_in[t % Y_BUFS][:, s, :, :], ALU.add).then_inc(y_added, 1)


def kernel(x, ctx_2048, L0_attn_Wq, L0_attn_bq, L0_attn_Wk, L0_attn_bk, L0_attn_Wv, L0_attn_bv,
           L0_attn_Wo, L0_attn_bo, L0_attn_slopes, L0_xattn_ssm_kernel, L0_xattn_D,
           L0_ffn_router_gate, L0_ffn_expert_gate_up, L0_ffn_expert_down):
    import numpy as np
    import concourse.bacc as bacc
    from concourse.bass_utils import run_bass_kernel_spmd

    B, T, E = x.shape
    n_experts, _, two_f = L0_ffn_expert_gate_up.shape
    laid_out = {
        "x": x,
        "ctx_t": np.transpose(ctx_2048, (2, 0, 1)).reshape(E // P, P, B * T)[:, ::-1].reshape(E, B * T),
        "wq_t": np.transpose(L0_attn_Wq), "bq": np.transpose(np.reshape(L0_attn_bq, (E // P, P))),
        "wk_t": np.transpose(L0_attn_Wk), "bk": np.transpose(np.reshape(L0_attn_bk, (E // P, P))),
        "wv_t": np.transpose(L0_attn_Wv), "bv": L0_attn_bv,
        "wo_t": np.transpose(L0_attn_Wo), "bo": L0_attn_bo,
        "slopes": L0_attn_slopes,
        "ssm_kernel": L0_xattn_ssm_kernel, "ssm_d": L0_xattn_D,
        "router_t": np.transpose(L0_ffn_router_gate),
        "gate_up": np.transpose(np.reshape(L0_ffn_expert_gate_up, (n_experts, E, two_f // 2, 2)), (0, 1, 3, 2)),
        "down": L0_ffn_expert_down,
    }
    nc = bacc.Bacc("TRN2", target_bir_lowering=False, num_devices=1)
    arrays, args = {}, []
    for name, a in laid_out.items():
        a = np.ascontiguousarray(a)
        arrays[f"in_{name}"] = a
        args.append(nc.dram_tensor(f"in_{name}", a.shape, mybir.dt.from_np(a.dtype), kind="ExternalInput").ap())
    args.append(nc.dram_tensor("out", (B, T, E), F32, kind="ExternalOutput").ap())
    build_decoder(nc, *args)
    r = run_bass_kernel_spmd(nc, [arrays], core_ids=[0])
    return r.results[0]["out"]
```

```python
from contextlib import ExitStack

import concourse.bass as bass
from concourse import mybir

F32 = mybir.dt.float32
F32R = mybir.dt.float32r
BF16 = mybir.dt.bfloat16
I32 = mybir.dt.int32
U32 = mybir.dt.uint32
ALU = mybir.AluOpType
ACT = mybir.ActivationFunctionType
AX_X = mybir.AxisListType.X

P = 128
EPS = 1e-5
ds = bass.ds
RSQRT_MAGIC = 1597463007.0
NEWTON_STEPS = 3
RSTD_OPS = 1 + 4 * NEWTON_STEPS


def wait_apart(engine, semaphore, value, passed):
    engine.wait_ge(semaphore, value)
    engine.sem_inc(passed, 1)


def reciprocal_sqrt(pool, out, variance, var_eps, scratch, step, count, done, passed):
    pool.tensor_scalar(var_eps, variance, EPS, None, ALU.add).then_inc(step, 1)
    wait_apart(pool, step, count + 1, passed)
    pool.tensor_scalar(out.bitcast(I32), var_eps.bitcast(I32), -0.5, RSQRT_MAGIC, ALU.mult, ALU.add).then_inc(step, 1)
    n = 2
    for i in range(NEWTON_STEPS):
        wait_apart(pool, step, count + n, passed)
        pool.tensor_tensor(scratch, var_eps, out, ALU.mult).then_inc(step, 1)
        wait_apart(pool, step, count + (n + 1), passed)
        pool.tensor_tensor(scratch, scratch, out, ALU.mult).then_inc(step, 1)
        wait_apart(pool, step, count + (n + 2), passed)
        pool.tensor_scalar(scratch, scratch, -0.5, 1.5, ALU.mult, ALU.add).then_inc(step, 1)
        wait_apart(pool, step, count + (n + 3), passed)
        last = pool.tensor_tensor(out, out, scratch, ALU.mult)
        n += 4
        if i < NEWTON_STEPS - 1:
            last.then_inc(step, 1)
    last.then_inc(done, 1)


def build_decoder(nc, x, ctx_t, wq_t, bq, wk_t, bk, wv_t, bv, wo_t, bo, slopes,
                  ssm_kernel, ssm_d, router_t, gate_up, down, out):
    B, T, E = x.shape
    H = slopes.shape[0]
    DH = E // H
    TT = T // P
    EC = E // P
    NT = B * TT
    HPC = P // DH
    Q_SCALE = DH ** -0.5
    SH = ssm_kernel.shape[0]
    SD = T // SH
    NE = router_t.shape[1]
    FI = down.shape[1]
    assert TT == 2 and EC == 4 and HPC == 4 and H == 16 and SD == 8 and B % 2 == 0

    x_tiles = x.rearrange("b (t p) e -> p (b t) e", p=P)
    out_tiles = out.rearrange("b (t p) e -> p (b t) e", p=P)

    with ExitStack() as whole:
        def sem(name):
            return whole.enter_context(nc.semaphore(name))

        def sbuf(name, shape, dt=F32, scope=whole):
            return scope.enter_context(nc.sbuf_tensor(name, shape, dt))

        def psum(name, shape, scope):
            return scope.enter_context(nc.psum_tensor(name, shape, F32))

        passed = sem("passed")
        ident = sbuf("ident", [P, P])
        all_stats = sbuf("all_stats", [P, NT, 6])
        all_moments = sbuf("all_moments", [P, NT, 2])
        all_rstd = sbuf("all_rstd", [P, NT])
        var_eps = sbuf("var_eps", [P, NT])
        newton = sbuf("newton", [P, NT])
        GB = B // 2
        GT = GB * TT
        with ExitStack() as last_of_all:
            w_gu_hi = sbuf("w_gu_hi", [P, NE, EC, 2 * FI], F32R, scope=last_of_all)
        with ExitStack() as later:
            x_res = sbuf("x_res", [P, NT, E], scope=later)
            ctx_g = sbuf("ctx_g", [P, EC, GB * T], scope=later)
        x1_load = [sem(f"x1_load{g}") for g in range(2)]
        ctx_load = sem("ctx_load")
        x1_rstd = sem("x1_rstd")
        ctx_view = ctx_t.rearrange("(m p) n -> p m n", p=P)
        x1_rows = nc.dram_tensor("x1_rows", [B * T, E], F32)
        x1_tiles = x1_rows.rearrange("(n p) e -> p n e", p=P)
        kernel_pad = nc.dram_tensor("kernel_pad", [SH, P + E], F32)

        N_TOK = B * T
        TOP = 2
        N_TILES = TOP * N_TOK // P + NE
        TOKEN, BACK, SCORE, PAIR_ROW = 0, 1, 2, 4
        NO_ROW = 1.0e6
        TABLE_ROWS = NE * N_TOK + NE * P
        row_table = nc.dram_tensor("row_table", [TABLE_ROWS, PAIR_ROW], F32)
        xn_rows = nc.dram_tensor("xn_rows", [N_TOK, E], F32)

        with ExitStack() as scope:
            def sb(name, shape, dt=F32):
                return sbuf(name, shape, dt, scope)

            WEIGHT_BUFS = 2
            wq, wk, wv = [[sb(f"{name}_{part}", [P, EC, E], F32R) for part in ("hi", "lo")]
                          for name in ("wq", "wk", "wv")]
            xn_t = [sb(f"xn_t_{part}", [P, EC, T], F32R) for part in ("hi", "lo")]
            w_in = [sb(f"w_in{i}", [P, 2, E]) for i in range(WEIGHT_BUFS)]
            q_hi, q_lo, k_hi, k_lo = [sb(name, [P, EC, T], F32R) for name in ("q_hi", "q_lo", "k_hi", "k_lo")]
            x_in = [sb(f"x_in{i}", [P, TT, E]) for i in range(2)]
            xn = sb("xn", [P, TT, E])
            free_rows = sb("free_rows", [P, TABLE_ROWS // P, PAIR_ROW])
            x1_stats_of = sb("x1_stats_of", [P, TT, 6])
            x1_moments_of = sb("x1_moments_of", [P, TT, 2])
            stats = sb("stats", [P, TT, 6])
            moments = sb("moments", [P, TT, 2])
            rstd = sb("rstd", [P, TT])
            x_mid = [sb(f"x_mid{i}", [P, TT, E]) for i in range(2)]
            wo = [sb(f"wo_{part}", [P, EC, E], F32R) for part in ("hi", "lo")]
            bq_col = sb("bq_col", [P, EC])
            bk_col = sb("bk_col", [P, EC])
            bv_row = sb("bv_row", [P, E])
            bo_row = sb("bo_row", [P, E])
            slope_row = sb("slope_row", [P, H])
            slope_scaled = sb("slope_scaled", [P, H])
            dist_i = sb("dist_i", [P, T + P], I32)
            dist = sb("dist", [P, T + P])
            dist_neg = sb("dist_neg", [P, T + P])
            alibi = [sb(f"alibi{i}", [P, T + P]) for i in range(2)]
            kernel_row = sb("kernel_row", [SH, P + E])
            d_col = sb("d_col", [SH, 1])
            q_stack = sb("q_stack", [3 * DH, HPC, EC, T], F32R)
            k_stack = sb("k_stack", [3 * DH, HPC, EC, T], F32R)
            v = [sb(f"v{i}", [P, TT, E]) for i in range(2)]
            neg_scores = [sb(f"neg_scores{i}", [P, TT, T]) for i in range(2)]
            probs = [sb(f"probs{i}", [P, TT, T]) for i in range(2)]
            probs_t = [sb(f"probs_t{i}", [P, TT, T]) for i in range(2)]
            neg_max = [sb(f"neg_max{i}", [P, H, TT]) for i in range(2)]
            row_sum = [sb(f"row_sum{i}", [P, TT, H]) for i in range(2)]
            inv_sum = sb("inv_sum", [P, TT, H])
            o_norm = sb("o_norm", [P, TT, E])
            o_t = [sb(f"o_t_{part}", [P, EC, T], F32R) for part in ("hi", "lo")]

            ps_scores = [psum(f"ps_scores{i}", [P, TT, T], scope) for i in range(2)]
            ps_probs_t = [psum(f"ps_probs_t{i}", [P, TT, T], scope) for i in range(2)]
            ps_o = psum("ps_o", [P, TT, E], scope)
            ps_proj = psum("ps_proj", [P, 2, E], scope)

            x_load = [sem(f"x_load{i}") for i in range(2)]
            x1_stored = [sem(f"x1_stored{i}") for i in range(2)]
            stack_load = [sem(f"stack_load{r}") for r in range(HPC)]
            w_load = [sem(f"w_in_load{i}") for i in range(WEIGHT_BUFS)]
            w_hi_ready = sem("w_hi_ready")
            w_ready = sem("w_ready")
            small_load = sem("small_load")
            kernel_store = sem("kernel_store")
            free_row_step = sem("free_row_step")
            free_rows_store = sem("free_rows_store")
            consts = sem("consts")
            alibi_step = sem("alibi_step")
            alibi_ready = sem("alibi_ready")
            kernel_ready = sem("kernel_ready")
            stats_ready = sem("stats_ready")
            moments_ready = sem("moments_ready")
            rstd_ready = sem("rstd_ready")
            rstd_step = sem("rstd_step")
            xn_ready = sem("xn_ready")
            bias_added = sem("bias_added")
            xt_done = sem("xt_done")
            xt_kept = sem("xt_kept")
            q_done = sem("q_done")
            q_kept = sem("q_kept")
            k_done = sem("k_done")
            k_kept = sem("k_kept")
            v_done = sem("v_done")
            v_kept = sem("v_kept")
            ot_done = sem("ot_done")
            ot_kept = sem("ot_kept")
            wo_done = sem("wo_done")
            x1_ready = sem("x1_ready")
            x1_stats = sem("x1_stats")
            x1_aggregated = sem("x1_aggregated")
            x1_moments = sem("x1_moments")
            x1_rstd_step = sem("x1_rstd_step")
            scores_ready = sem("scores_ready")
            max_ready = sem("max_ready")
            probs_ready = sem("probs_ready")
            probs_t_ready = sem("probs_t_ready")
            probs_t_kept = [sem(f"probs_t_kept{i}") for i in range(2)]
            pv_ready = sem("pv_ready")
            inv_ready = sem("inv_ready")
            o_kept = sem("o_kept")

            def after(k, par):
                return (k, 1) if par == 0 else (k + 1, 0)

            def before(k, par):
                return (k, 0) if par == 1 else (k - 1, 1)

            def batch(k, par):
                return k * 2 + par

            def head(k, par, h):
                return k * (2 * H) + (par * H + h)

            HEADS = [c * HPC + r for r in range(HPC) for c in range(EC)]
            O_SLOTS, Q_SLOTS, K_SLOTS, V_SLOTS = (2, 2, 3, 4), (5, 6, 6, 7), (8, 8, 9, 10), (11, 12, 13, 14)
            VECTOR_HEADS = (1, 5, 9, 13)
            STACK_LOADS = 6 * 16

            def is_first(k, par, h=0):
                return isinstance(k, int) and k == 0 and par == 0 and h < 2

            def steps(eng, emit):
                emit(0, 0, False, True)
                with eng.Fori(0, B // 2 - 1) as k:
                    emit(k, 1, True, True)
                    emit(k + 1, 0, True, True)
                emit(B // 2 - 1, 1, True, False)

            block = scope.enter_context(nc.Block())

            @block.sync
            def _(sp):
                def load_x(k, par):
                    b = batch(k, par)
                    if not (isinstance(k, int) and k == 0):
                        sp.wait_ge(xn_ready, b * TT - TT)
                        sp.wait_ge(bias_added, b * TT - TT)
                    sp.dma_start(x_in[par][:], x_tiles[:, ds(b * TT, TT), :]).then_inc(x_load[par], 16)

                def store_x1(k, par):
                    b = batch(k, par)
                    sp.wait_ge(x1_ready, b * TT + TT)
                    sp.dma_start(x1_tiles[:, ds(b * TT, TT), :], x_mid[par][:]).then_inc(x1_stored[par], 16)

                load_x(0, 0)
                load_x(0, 1)
                n = 0
                for src in (wq_t, wk_t, wv_t, wo_t):
                    for half in range(2):
                        if n >= WEIGHT_BUFS:
                            sp.wait_ge(w_ready, n + 1 - WEIGHT_BUFS)
                        sp.dma_start(w_in[n % WEIGHT_BUFS][:],
                                     src.rearrange("(h c p) f -> h p c f", h=2, p=P)[half]).then_inc(w_load[n % WEIGHT_BUFS], 16)
                        n += 1
                load_x(1, 0)
                load_x(1, 1)
                sp.wait_ge(free_row_step, 2)
                sp.dma_start(row_table.rearrange("(p k) c -> p k c", p=P), free_rows[:]).then_inc(free_rows_store, 16)
                sp.wait_ge(kernel_ready, 3)
                sp.dma_start(kernel_pad[:, :], kernel_row[:]).then_inc(kernel_store, 16)
                with sp.Fori(2, B // 2) as k:
                    for par in range(2):
                        store_x1(k - 2, par)
                        load_x(k, par)
                for par in range(2):
                    store_x1(B // 2 - 2, par)
                sp.wait_ge(v_done, B * TT)
                sp.wait_ge(bias_added, B * TT)
                for r in range(HPC):
                    sp.wait_ge(stack_load[r], B * STACK_LOADS)
                for par in range(2):
                    sp.wait_ge(x1_stored[par], GB // 2 * 16)
                sp.wait_ge(free_rows_store, 16)
                sp.dma_start(ctx_g[:], ctx_view[:, :, 0:GB * T]).then_inc(ctx_load, 16)
                sp.dma_start(x_res[:, 0:GT, :], x1_tiles[:, 0:GT, :]).then_inc(x1_load[0], 16)
                for par in range(2):
                    store_x1(B // 2 - 1, par)
                for par in range(2):
                    sp.wait_ge(x1_stored[par], B // 2 * 16)
                sp.wait_ge(kernel_store, 16)

            @block.gpsimd
            def _(pool):
                pool.memset(ident[:], 0.0).then_inc(consts, 1)
                pool.wait_ge(consts, 1)
                pool.affine_select(out=ident[:], in_=ident[:], compare_op=ALU.not_equal, fill=1.0, base=0,
                                   pattern=[[-1, P]], channel_multiplier=1).then_inc(consts, 1)
                pool.iota(dist_i[:], pattern=[[-1, T + P]], base=P, channel_multiplier=1).then_inc(consts, 1)
                pool.memset(kernel_row[:, 0:P], 0.0).then_inc(kernel_ready, 1)
                pool.memset(free_rows[:], 0.0).then_inc(free_row_step, 1)
                pool.wait_ge(free_row_step, 1)
                pool.memset(free_rows[:, :, BACK:BACK + 1], NO_ROW).then_inc(free_row_step, 1)

                def rstd_of(k, par):
                    wait_apart(pool, moments_ready, batch(k, par) * TT + TT, passed)
                    reciprocal_sqrt(pool, rstd[:], moments[:, :, 1], var_eps[:, 0:TT], newton[:, 0:TT], rstd_step,
                                    batch(k, par) * RSTD_OPS, rstd_ready, passed)

                def add_output_bias(k, par):
                    b = batch(k, par)
                    pool.wait_ge(small_load, 16 * 7)
                    wait_apart(pool, xn_ready, b * TT + TT, passed)
                    if not (isinstance(k, int) and k == 0):
                        wait_apart(pool, x1_stored[par], k * 16, passed)
                        wait_apart(pool, x1_stats, b * TT - TT, passed)
                    for tt in range(TT):
                        pool.tensor_tensor(x_mid[par][:, tt, :], x_in[par][:, tt, :], bo_row[:], ALU.add)\
                            .then_inc(bias_added, 1)

                def stack(k, par, r, q_part):
                    b = batch(k, par)
                    wait_apart(pool, q_kept if q_part else k_kept, b * (2 * EC) + 2 * EC, passed)
                    if not is_first(k, par):
                        wait_apart(pool, scores_ready, head(k, par, r * EC) + EC - H, passed)
                    to, parts = (q_stack, (q_hi, q_lo, q_hi)) if q_part else (k_stack, (k_hi, k_hi, k_lo))
                    for n, part in enumerate(parts):
                        pool.dma_start(to[n * DH:n * DH + DH, r, :, :], part[r * DH:r * DH + DH, :, :])\
                            .then_inc(stack_load[r], 16)

                STACK_ORDER = [(0, True), (1, True), (2, True), (0, False), (1, False), (2, False), (3, True), (3, False)]
                STACK_SLOTS = (8, 9, 10, 11, 12, 13, 14, 15)

                rstd_of(0, 0)
                rstd_of(0, 1)
                add_output_bias(0, 0)
                for r in range(HPC):
                    for q_part in (True, False):
                        stack(0, 0, r, q_part)

                def step(k, par, has_before, has_after):
                    for i in range(H):
                        if has_before and has_after and i == 1:
                            rstd_of(*after(k, par))
                        if has_after and i == 7:
                            add_output_bias(*after(k, par))
                        if has_after and i in STACK_SLOTS:
                            stack(*after(k, par), *STACK_ORDER[STACK_SLOTS.index(i)])

                steps(pool, step)
                pool.wait_ge(x1_moments, GB)
                reciprocal_sqrt(pool, all_rstd[:, 0:GT], all_moments[:, 0:GT, 1], var_eps[:, 0:GT], newton[:, 0:GT],
                                x1_rstd_step, 0, x1_rstd, passed)

            @block.tensor
            def _(pe):
                def x_transposes(k, par, bank_read, read):
                    b = batch(k, par)
                    pe.wait_ge(xn_ready, b * TT + TT)
                    for half in range(2):
                        if bank_read is not None:
                            pe.wait_ge(bank_read, read + half)
                        for c in range(2):
                            for tt in range(TT):
                                e = 2 * half + c
                                last = pe.transpose(ps_proj[:, half, c * T + tt * P:c * T + tt * P + P],
                                                    xn[:, tt, e * P:e * P + P], ident[:])
                        last.then_inc(xt_done, 1)

                PARTS = ((0, 0), (0, 1), (1, 0))

                def q_or_k(k, par, half, c, w, done):
                    b = batch(k, par)
                    if c == 0 and w is wq:
                        pe.wait_ge(xt_kept, b * 4 + 4)
                    elif c == 0:
                        pe.wait_ge(q_kept, b * (2 * EC) + (4 * half + 4))
                    f = 2 * half + c
                    for e in range(EC):
                        for w_part, x_part in PARTS:
                            last = pe.matmul(ps_proj[:, half, c * T:c * T + T], w[w_part][:, e, f * P:f * P + P],
                                             xn_t[x_part][:, e, :], start=(e == 0 and w_part == x_part == 0),
                                             stop=(e == EC - 1 and w_part == 1))
                    if c == 1:
                        last.then_inc(done, 1)

                def token_rows(rows, w, tt, piece):
                    for e in (2 * piece, 2 * piece + 1):
                        for x_part, w_part in PARTS:
                            last = pe.matmul(ps_proj[:, tt, :], rows[x_part][:, e, tt * P:tt * P + P], w[w_part][:, e, :],
                                             start=(e == 0 and w_part == x_part == 0),
                                             stop=(e == EC - 1 and x_part == 1))
                    return last

                def v_rows(k, par, tt, piece):
                    if piece == 0:
                        pe.wait_ge(k_kept, batch(k, par) * (2 * EC) + (4 * tt + 4))
                    last = token_rows(xn_t, wv, tt, piece)
                    if piece == 1:
                        last.then_inc(v_done, 1)

                def o_transposes(k, par, v_read):
                    pe.wait_ge(o_kept, batch(k, par) * TT + TT)
                    for half in range(2):
                        if v_read is not None:
                            pe.wait_ge(v_kept, v_read + half)
                        for c in range(2):
                            for tt in range(TT):
                                e = 2 * half + c
                                last = pe.transpose(ps_proj[:, half, c * T + tt * P:c * T + tt * P + P],
                                                    o_norm[:, tt, e * P:e * P + P], ident[:])
                        last.then_inc(ot_done, 1)

                def output_rows(k, par, tt, piece):
                    if piece == 0:
                        pe.wait_ge(ot_kept, batch(k, par) * 4 + 4)
                    last = token_rows(o_t, wo, tt, piece)
                    if piece == 1:
                        last.then_inc(wo_done, 1)

                def scores(k, par, h):
                    b = batch(k, par)
                    r, c = h // EC, h % EC
                    if c == 0:
                        pe.wait_ge(stack_load[r], b * STACK_LOADS + STACK_LOADS)
                    if not is_first(k, par, h):
                        pe.wait_ge(max_ready, head(k, par, h) - 1)
                    for tt in range(TT):
                        last = pe.matmul(ps_scores[h % 2][:, tt, :], q_stack[:, r, c, tt * P:tt * P + P],
                                         k_stack[:, r, c, :], start=True, stop=True)
                    last.then_inc(scores_ready, 1)

                def probs_transposes(k, par, h):
                    pe.wait_ge(probs_ready, head(k, par, h) + 1)
                    if not is_first(k, par, h):
                        pe.wait_ge(probs_t_kept[h % 2], batch(k, par) * (H // 2) + h // 2)
                    for jt in range(TT):
                        for tt in range(TT):
                            last = pe.transpose(ps_probs_t[h % 2][:, jt, tt * P:tt * P + P],
                                                probs[h % 2][:, tt, jt * P:jt * P + P], ident[:])
                    last.then_inc(probs_t_ready, 1)

                def pv(k, par, h):
                    b = batch(k, par)
                    if h == 0:
                        pe.wait_ge(v_kept, b * TT + TT)
                        if not is_first(k, par):
                            pe.wait_ge(o_kept, b * TT)
                    pe.wait_ge(probs_t_kept[h % 2], b * (H // 2) + (h // 2 + 1))
                    features = slice(HEADS[h] * DH, HEADS[h] * DH + DH)
                    for tt in range(TT):
                        for jt in range(TT):
                            last = pe.matmul(ps_o[:, tt, features], probs_t[h % 2][:, jt, tt * P:tt * P + P],
                                             v[par][:, jt, features], start=(jt == 0), stop=(jt == TT - 1))
                    last.then_inc(pv_ready, 1)

                def step(k, par, has_before, has_after):
                    b, prev, nxt = batch(k, par), before(k, par), after(k, par)
                    for h in range(H):
                        if h + 2 < H:
                            scores(k, par, h + 2)
                        elif has_after:
                            scores(*nxt, h + 2 - H)
                        if has_before and h == 1:
                            o_transposes(*prev, b * TT + 1)
                        for n, slot in enumerate(O_SLOTS):
                            if has_before and h == slot:
                                output_rows(*prev, n // 2, n % 2)
                        if has_after and h == O_SLOTS[-1]:
                            if has_before:
                                x_transposes(*nxt, x1_ready, b * TT - TT + 1)
                            else:
                                x_transposes(*nxt, v_kept, 1)
                        if has_after:
                            for n in range(4):
                                if h == Q_SLOTS[n]:
                                    q_or_k(*nxt, n // 2, n % 2, wq, q_done)
                                if h == K_SLOTS[n]:
                                    q_or_k(*nxt, n // 2, n % 2, wk, k_done)
                                if h == V_SLOTS[n]:
                                    v_rows(*nxt, n // 2, n % 2)
                        probs_transposes(k, par, h)
                        if h:
                            pv(k, par, h - 1)
                        elif has_before:
                            pv(*prev, H - 1)

                pe.wait_ge(consts, 2)
                x_transposes(0, 0, None, 0)
                for w, done, halves in ((wq, q_done, 2), (wk, k_done, 4)):
                    pe.wait_ge(w_ready, halves)
                    for n in range(4):
                        q_or_k(0, 0, n // 2, n % 2, w, done)
                pe.wait_ge(w_ready, 6)
                for n in range(4):
                    v_rows(0, 0, n // 2, n % 2)
                pe.wait_ge(w_ready, 8)
                scores(0, 0, 0)
                scores(0, 0, 1)
                steps(pe, step)
                pv(B // 2 - 1, 1, H - 1)
                o_transposes(B // 2 - 1, 1, None)
                for n in range(4):
                    output_rows(B // 2 - 1, 1, n // 2, n % 2)

            @block.vector
            def _(dve):
                def token_stats(k, par):
                    dve.wait_ge(x_load[par], k * 16 + 16)
                    for tt in range(TT):
                        dve.bn_stats(stats[:, tt, :], x_in[par][:, tt, :]).then_inc(stats_ready, 1)

                def token_moments(k, par):
                    wait_apart(dve, stats_ready, batch(k, par) * TT + TT, passed)
                    for tt in range(TT):
                        dve.bn_aggr(moments[:, tt, :], stats[:, tt, :]).then_inc(moments_ready, 1)

                def normalise(k, par, tt):
                    dve.wait_ge(rstd_ready, batch(k, par) + 1)
                    dve.tensor_scalar(xn[:, tt, :], x_in[par][:, tt, :], moments[:, tt, 0:1], rstd[:, tt:tt + 1],
                                      ALU.subtract, ALU.mult).then_inc(xn_ready, 1)

                def keep_t_lo(k, par, to, kept):
                    for half in range(2):
                        dve.wait_ge(kept, batch(k, par) * 4 + (2 * half + 1))
                        dve.tensor_tensor(to[1][:, 2 * half:2 * half + 2, :],
                                          ps_proj[:, half, :].rearrange("p (c t) -> p c t", t=T),
                                          to[0][:, 2 * half:2 * half + 2, :], ALU.subtract).then_inc(kept, 1)

                def keep_q_lo(k, par, half):
                    n = batch(k, par) * (2 * EC) + half * 4
                    for c in range(2):
                        f = 2 * half + c
                        dve.wait_ge(q_kept, n + (2 + c))
                        dve.scalar_tensor_tensor(q_lo[:, f, :], ps_proj[:, half, c * T:c * T + T], bq_col[:, f:f + 1],
                                                 q_hi[:, f, :], ALU.add, ALU.subtract).then_inc(q_kept, 1)

                def keep_k_lo(k, par, half):
                    n = batch(k, par) * (2 * EC) + half * 4
                    for c in range(2):
                        f = 2 * half + c
                        dve.wait_ge(k_kept, n + (2 + c))
                        dve.scalar_tensor_tensor(k_lo[:, f, :], ps_proj[:, half, c * T:c * T + T], bk_col[:, f:f + 1],
                                                 k_hi[:, f, :], ALU.add, ALU.subtract).then_inc(k_kept, 1)

                def keep_v(k, par, tt):
                    dve.wait_ge(v_done, batch(k, par) * TT + (tt + 1))
                    dve.tensor_tensor(v[par][:, tt, :], ps_proj[:, tt, :], bv_row[:], ALU.add).then_inc(v_kept, 1)

                def head_alibi(k, par, h):
                    if not is_first(k, par, h):
                        dve.wait_ge(max_ready, head(k, par, h) - 1)
                    dve.tensor_scalar(alibi[h % 2][:], dist_neg[:], slope_scaled[:, HEADS[h]:HEADS[h] + 1], None,
                                      ALU.mult).then_inc(alibi_ready, 1)

                def score_max(k, par, h):
                    g = head(k, par, h)
                    if not is_first(k, par, h):
                        dve.wait_ge(probs_ready, g - 1)
                    dve.wait_ge(alibi_ready, g + 1)
                    wait_apart(dve, scores_ready, g + 1, passed)
                    for tt in range(TT):
                        last = dve.tensor_tensor_reduce(neg_scores[h % 2][:, tt, :], ps_scores[h % 2][:, tt, :],
                                                        alibi[h % 2][:, P - P * tt:P - P * tt + T], -Q_SCALE, 3e38,
                                                        ALU.add, ALU.min, neg_max[par][:, h, tt:tt + 1])
                    last.then_inc(max_ready, 1)

                def keep_probs_t(k, par, h):
                    g = head(k, par, h)
                    dve.wait_ge(probs_t_ready, g + 1)
                    if not is_first(k, par, h):
                        dve.wait_ge(pv_ready, g - 1)
                    dve.tensor_copy(probs_t[h % 2][:], ps_probs_t[h % 2][:]).then_inc(probs_t_kept[h % 2], 1)

                def keep_o(k, par):
                    b = batch(k, par)
                    dve.wait_ge(pv_ready, b * H + H)
                    dve.reciprocal(inv_sum[:], row_sum[par][:]).then_inc(inv_ready, 1)
                    dve.wait_ge(inv_ready, b + 1)
                    for tt in range(TT):
                        dve.tensor_tensor(o_norm[:, tt, :].rearrange("p (h d) -> p h d", d=DH),
                                          ps_o[:, tt, :].rearrange("p (h d) -> p h d", d=DH),
                                          inv_sum[:, tt, :].unsqueeze(2).to_broadcast([P, H, DH]),
                                          ALU.mult).then_inc(o_kept, 1)

                def add_attention(k, par, tt):
                    b = batch(k, par)
                    dve.wait_ge(wo_done, b * TT + (tt + 1))
                    dve.wait_ge(bias_added, b * TT + TT)
                    dve.tensor_tensor(x_mid[par][:, tt, :], ps_proj[:, tt, :], x_mid[par][:, tt, :],
                                      ALU.add).then_inc(x1_ready, 1)

                def x1_statistics(k, par):
                    b = batch(k, par)
                    dve.wait_ge(x1_ready, b * TT + TT)
                    for tt in range(TT):
                        dve.bn_stats(x1_stats_of[:, tt, :], x_mid[par][:, tt, :]).then_inc(x1_stats, 1)
                    wait_apart(dve, x1_stats, b * TT + TT, passed)
                    for tt in range(TT):
                        dve.bn_aggr(x1_moments_of[:, tt, :], x1_stats_of[:, tt, :]).then_inc(x1_aggregated, 1)
                    dve.wait_ge(x1_aggregated, b * TT + TT)
                    dve.tensor_copy(all_moments[:, ds(b * TT, TT), :], x1_moments_of[:]).then_inc(x1_moments, 1)

                def step(k, par, has_before, has_after):
                    prev, nxt = before(k, par), after(k, par)
                    for h in range(H):
                        if h == 0 and has_before and H - 1 in VECTOR_HEADS:
                            keep_probs_t(*prev, H - 1)
                        if h and h - 1 in VECTOR_HEADS:
                            keep_probs_t(k, par, h - 1)
                        if h + 1 < H:
                            score_max(k, par, h + 1)
                        elif has_after:
                            score_max(*nxt, 0)
                        if h + 2 < H:
                            head_alibi(k, par, h + 2)
                        elif has_after:
                            head_alibi(*nxt, h + 2 - H)
                        if has_before and h == 0:
                            keep_o(*prev)
                        if has_before and h == 1:
                            keep_t_lo(*prev, o_t, ot_kept)
                        if has_before and h in (O_SLOTS[1], O_SLOTS[3]):
                            add_attention(*prev, O_SLOTS.index(h) // 2)
                        if has_before and h == O_SLOTS[3] + 1:
                            x1_statistics(*prev)
                        if has_after:
                            if h == 0 and has_before:
                                token_stats(*nxt)
                                token_moments(*nxt)
                            if h in (2, 3):
                                normalise(*nxt, h - 2)
                            if h == O_SLOTS[-1]:
                                keep_t_lo(*nxt, xn_t, xt_kept)
                            for half in range(2):
                                if h == Q_SLOTS[2 * half + 1]:
                                    keep_q_lo(*nxt, half)
                                if h == K_SLOTS[2 * half + 1]:
                                    keep_k_lo(*nxt, half)
                                if h == V_SLOTS[2 * half + 1]:
                                    keep_v(*nxt, half)

                token_stats(0, 0)
                token_moments(0, 0)
                for tt in range(TT):
                    normalise(0, 0, tt)
                halves = [(w, half) for w in (wq, wk, wv, wo) for half in range(2)]

                def split_lo(n):
                    w, half = halves[n]
                    dve.wait_ge(w_hi_ready, n + 1)
                    dve.tensor_tensor(w[1][:, 2 * half:2 * half + 2, :], w_in[n % WEIGHT_BUFS][:],
                                      w[0][:, 2 * half:2 * half + 2, :], ALU.subtract).then_inc(w_ready, 1)

                token_stats(0, 1)
                token_moments(0, 1)
                split_lo(0)
                split_lo(1)
                keep_t_lo(0, 0, xn_t, xt_kept)
                split_lo(2)
                split_lo(3)
                dve.wait_ge(consts, 3)
                dve.wait_ge(small_load, 16 * 7)
                dve.tensor_copy(dist[:], dist_i[:]).then_inc(alibi_step, 1)
                dve.wait_ge(alibi_step, 1)
                dve.tensor_scalar(dist_neg[:], dist[:], -1.0, None, ALU.mult).then_inc(alibi_step, 1)
                dve.wait_ge(alibi_step, 2)
                dve.tensor_tensor(dist_neg[:], dist_neg[:], dist[:], ALU.min).then_inc(alibi_step, 1)
                dve.tensor_scalar(slope_scaled[:], slope_row[:], 1 / Q_SCALE, None, ALU.mult).then_inc(alibi_step, 1)
                dve.tensor_tensor(kernel_row[:, P:P + 1], kernel_row[:, P:P + 1], d_col[:],
                                  ALU.add).then_inc(kernel_ready, 2)
                for half in range(2):
                    keep_q_lo(0, 0, half)
                split_lo(4)
                split_lo(5)
                for half in range(2):
                    keep_k_lo(0, 0, half)
                for tt in range(TT):
                    keep_v(0, 0, tt)
                split_lo(6)
                split_lo(7)
                dve.wait_ge(alibi_step, 4)
                head_alibi(0, 0, 0)
                head_alibi(0, 0, 1)
                score_max(0, 0, 0)
                steps(dve, step)
                last = (B // 2 - 1, 1)
                if H - 1 in VECTOR_HEADS:
                    keep_probs_t(*last, H - 1)
                keep_o(*last)
                keep_t_lo(*last, o_t, ot_kept)
                for tt in range(TT):
                    add_attention(*last, tt)
                x1_statistics(*last)

            @block.scalar
            def _(act):
                def keep_t_hi(k, par, to, done, kept):
                    for half in range(2):
                        act.wait_ge(done, batch(k, par) * 2 + (half + 1))
                        if half:
                            act.wait_ge(kept, batch(k, par) * 4 + 2)
                        act.activation(to[0][:, 2 * half:2 * half + 2, :], ps_proj[:, half, :], ACT.Copy)\
                            .then_inc(kept, 1)

                def keep_q_hi(k, par, half):
                    act.wait_ge(q_done, batch(k, par) * 2 + (half + 1))
                    if half == 0 and not is_first(k, par):
                        for r in range(HPC):
                            act.wait_ge(stack_load[r], batch(k, par) * STACK_LOADS)
                    if half:
                        act.wait_ge(q_kept, batch(k, par) * (2 * EC) + 4)
                    for c in range(2):
                        f = 2 * half + c
                        act.activation(q_hi[:, f, :], ps_proj[:, half, c * T:c * T + T], ACT.Identity,
                                       bias=bq_col[:, f:f + 1]).then_inc(q_kept, 1)

                def keep_k_hi(k, par, half):
                    act.wait_ge(k_done, batch(k, par) * 2 + (half + 1))
                    if half == 0 and not is_first(k, par):
                        for r in range(HPC):
                            act.wait_ge(stack_load[r], batch(k, par) * STACK_LOADS)
                    if half:
                        act.wait_ge(k_kept, batch(k, par) * (2 * EC) + 4)
                    for c in range(2):
                        f = 2 * half + c
                        act.activation(k_hi[:, f, :], ps_proj[:, half, c * T:c * T + T], ACT.Identity,
                                       bias=bk_col[:, f:f + 1]).then_inc(k_kept, 1)

                def exponentials(k, par, h):
                    g = head(k, par, h)
                    act.wait_ge(max_ready, g + 1)
                    if not is_first(k, par, h):
                        act.wait_ge(probs_t_ready, g - 1)
                    for tt in range(TT):
                        last = act.activation(probs[h % 2][:, tt, :], neg_scores[h % 2][:, tt, :], ACT.Exp,
                                              bias=neg_max[par][:, h, tt:tt + 1], scale=-1.0,
                                              accum_out=row_sum[par][:, tt, HEADS[h]:HEADS[h] + 1])
                    last.then_inc(probs_ready, 1)

                def keep_probs_t(k, par, h):
                    g = head(k, par, h)
                    act.wait_ge(probs_t_ready, g + 1)
                    if not is_first(k, par, h):
                        act.wait_ge(pv_ready, g - 1)
                    act.activation(probs_t[h % 2][:], ps_probs_t[h % 2][:], ACT.Copy).then_inc(probs_t_kept[h % 2], 1)

                def step(k, par, has_before, has_after):
                    prev, nxt = before(k, par), after(k, par)
                    for h in range(H):
                        if h == 0 and has_before and H - 1 not in VECTOR_HEADS:
                            keep_probs_t(*prev, H - 1)
                        if h and h - 1 not in VECTOR_HEADS:
                            keep_probs_t(k, par, h - 1)
                        if has_before and h == 1:
                            keep_t_hi(*prev, o_t, ot_done, ot_kept)
                        if h + 1 < H:
                            exponentials(k, par, h + 1)
                        elif has_after:
                            exponentials(*nxt, 0)
                        if has_after and h == O_SLOTS[-1]:
                            keep_t_hi(*nxt, xn_t, xt_done, xt_kept)
                        for half in range(2):
                            if has_after and h == Q_SLOTS[2 * half + 1]:
                                keep_q_hi(*nxt, half)
                            if has_after and h == K_SLOTS[2 * half + 1]:
                                keep_k_hi(*nxt, half)

                for dst, src in ((bq_col, bq), (bk_col, bk)):
                    act.dma_start(dst[:], src).then_inc(small_load, 16)
                for dst, src in ((bv_row, bv), (bo_row, bo), (slope_row, slopes)):
                    act.dma_start(dst[:], src.partition_broadcast(P)).then_inc(small_load, 16)
                act.dma_start(d_col[:], ssm_d.rearrange("(h o) -> h o", o=1)).then_inc(small_load, 16)
                act.dma_start(kernel_row[:, P:], ssm_kernel).then_inc(small_load, 16)
                halves = [(w, half) for w in (wq, wk, wv, wo) for half in range(2)]

                def split_hi(n):
                    w, half = halves[n]
                    act.wait_ge(w_load[n % WEIGHT_BUFS], n // WEIGHT_BUFS * 16 + 16)
                    act.activation(w[0][:, 2 * half:2 * half + 2, :], w_in[n % WEIGHT_BUFS][:], ACT.Copy)\
                        .then_inc(w_hi_ready, 1)

                split_hi(0)
                split_hi(1)
                keep_t_hi(0, 0, xn_t, xt_done, xt_kept)
                split_hi(2)
                split_hi(3)
                act.wait_ge(small_load, 16 * 7)
                for half in range(2):
                    keep_q_hi(0, 0, half)
                split_hi(4)
                split_hi(5)
                for half in range(2):
                    keep_k_hi(0, 0, half)
                split_hi(6)
                split_hi(7)
                exponentials(0, 0, 0)
                steps(act, step)
                if H - 1 not in VECTOR_HEADS:
                    keep_probs_t(B // 2 - 1, 1, H - 1)
                keep_t_hi(B // 2 - 1, 1, o_t, ot_done, ot_kept)


        PAIRS = SD * (SD + 1) // 2
        TAP_BUFS = 4
        FOLD = 2

        def pair_segments():
            segments = [(0, 0, 0, SD)]
            for d in range(1, SD // 2):
                segments += [(d * SD, 0, d, SD - d), (d * SD + SD - d, SD - d, 0, d)]
            return segments + [(SD // 2 * SD, 0, SD // 2, SD // 2)]

        with ExitStack() as scope:
            def sb(name, shape, dt=F32):
                return sbuf(name, shape, dt, scope)

            sbuf("x_res_place", [P, NT, E])
            sb("ctx_g_place", [P, EC, GB * T])
            q_g = sb("q_g", [P, EC, GB * T])
            taps = [sb(f"taps{i}", [P, E]) for i in range(TAP_BUFS)]
            pairs = [sb(f"pairs{i}", [P, EC, GB, PAIRS]) for i in range(2)]
            prods = [sb(f"prods{i}", [P, EC, GB, SD, SD]) for i in range(2)]
            xn_g = [sb(f"xn_g{i}", [P, TT, E]) for i in range(2)]
            ps_y = [psum(f"ps_y{i}", [P, EC, E], scope) for i in range(2)]

            tap_load = [sem(f"tap_load{i}") for i in range(TAP_BUFS)]
            c_rstd_step = sem("c_rstd_step")
            c_rstd = sem("c_rstd")
            c_xn = sem("c_xn")
            c_xt_done = sem("c_xt_done")
            c_xt_kept = sem("c_xt_kept")
            pairs_ready = sem("pairs_ready")
            y_ready = sem("y_ready")
            prods_ready = sem("prods_ready")
            folded = sem("folded")
            z_ready = sem("z_ready")
            zt_done = sem("zt_done")
            x2_ready = sem("x2_ready")
            x2_stats = sem("x2_stats")
            x2_moments = sem("x2_moments")
            x2_rstd_step = sem("x2_rstd_step")
            x2_rstd = sem("x2_rstd")
            Y_START, PRODS_START, XT_START, X2_START = TAP_BUFS, 2, 2, 8
            Z_START, XT_DONE_START = 2, 2

            def by_head(tile):
                return tile[:, :, :].rearrange("p m (b s i) -> p m b s i", b=GB, s=SH)

            def head_of(tile, h, i, n):
                v = by_head(tile)[:, :, :, ds(h, 1), i:i + n]
                return v.rearrange("p m b s i -> p m b (s i)")

            skewed = bass.AP(tensor=kernel_pad, offset=1, ap=[[P + E, SH], [1, P], [1, E]])

            block = scope.enter_context(nc.Block())

            @block.sync
            def _(sp):
                for g in range(2):
                    if g:
                        sp.wait_ge(pairs_ready, SH)
                        sp.dma_start(ctx_g[:], ctx_view[:, :, GB * T:]).then_inc(ctx_load, 16)
                    with sp.Fori(0, SH // TAP_BUFS) as k:
                        for r in range(TAP_BUFS):
                            sp.wait_ge(y_ready, k * TAP_BUFS + (g * SH + r + 1 - TAP_BUFS + Y_START))
                            sp.dma_start(taps[r][:], skewed[ds(k * TAP_BUFS + r, 1), :, :].rearrange("o p c -> p (o c)"))\
                                .then_inc(tap_load[r], 16)

            @block.gpsimd
            def _(pool):
                def form_pairs(g, k, par):
                    pool.wait_ge(y_ready, k * 2 + (g * SH + par + 1 - 2 + Y_START))
                    for col, i, j, n in pair_segments():
                        last = pool.tensor_tensor(pairs[par][:, :, :, col:col + n],
                                                  head_of(ctx_g, k * 2 + par, i, n),
                                                  head_of(ctx_g, k * 2 + par, j, n), ALU.mult)
                    last.then_inc(pairs_ready, 1)

                def fold(g, k, par):
                    wait_apart(pool, prods_ready, k * 2 + (g * SH + par + 1 + PRODS_START), passed)
                    first = prods[par][:, :, :, :, 0:FOLD]
                    pool.tensor_tensor(first, first, prods[par][:, :, :, :, SD - FOLD:SD], ALU.add).then_inc(folded, 1)

                for g in range(2):
                    pool.wait_ge(ctx_load, 16 * g + 16)
                    for par in range(2):
                        form_pairs(g, 0, par)
                    if g == 0:
                        reciprocal_sqrt(pool, all_rstd[:, GT:NT], all_moments[:, GT:NT, 1], var_eps[:, GT:NT],
                                        newton[:, GT:NT], c_rstd_step, 0, c_rstd, passed)
                    with pool.Fori(1, SH // 2) as k:
                        for par in range(2):
                            form_pairs(g, k, par)
                            fold(g, k - 1, par)
                    for par in range(2):
                        fold(g, SH // 2 - 1, par)
                pool.wait_ge(x2_moments, GT)
                reciprocal_sqrt(pool, all_rstd[:, 0:GT], all_moments[:, 0:GT, 1], var_eps[:, 0:GT],
                                newton[:, 0:GT], x2_rstd_step, 0, x2_rstd, passed)

            @block.tensor
            def _(pe):
                pe.sem_inc(y_ready, Y_START)
                pe.sem_inc(c_xt_done, XT_DONE_START)

                def x_transposes(g, k, par):
                    n = k * 2 + (par + g * GB)
                    pe.wait_ge(c_xn, n * TT + TT)
                    pe.wait_ge(c_xt_kept, n + (1 - 2 + XT_START))
                    for c in range(EC):
                        for tt in range(TT):
                            last = pe.transpose(ps_y[par][:, c, tt * P:tt * P + P], xn_g[par][:, tt, c * P:c * P + P],
                                                ident[:])
                    last.then_inc(c_xt_done, 1)

                def convolve(g, k, r):
                    h = k * TAP_BUFS + (r + g * SH)
                    par = r % 2
                    pe.wait_ge(pairs_ready, h + 1)
                    pe.wait_ge(tap_load[r], k * 16 + (g * (SH // TAP_BUFS) * 16 + 16))
                    pe.wait_ge(prods_ready, h + (1 - 2 + PRODS_START))
                    for lc in range(EC):
                        for mc in range(lc + 1):
                            block_cols = (lc - mc) * P
                            last = pe.matmul(ps_y[par][:, lc, 0:GB * PAIRS], taps[r][:, block_cols:block_cols + P],
                                             pairs[par][:, mc, :, :], start=(mc == 0), stop=(mc == lc))
                    last.then_inc(y_ready, 1)

                for g in range(2):
                    if g:
                        pe.wait_ge(x2_ready, GT + X2_START)
                    with pe.Fori(0, GB // 2) as k:
                        for par in range(2):
                            x_transposes(g, k, par)
                    pe.wait_ge(c_xt_kept, (g + 1) * GB + XT_START)
                    with pe.Fori(0, SH // TAP_BUFS) as k:
                        for r in range(TAP_BUFS):
                            convolve(g, k, r)
                    pe.wait_ge(z_ready, (g + 1) * SH + Z_START)
                    for t in range(GT):
                        bank = ps_y[t % 8 // EC][:, t % EC, :]
                        pe.wait_ge(x2_ready, g * GT + t + 1 - 8 + X2_START)
                        for c in range(EC):
                            last = pe.transpose(bank[:, c * P:c * P + P], q_g[:, c, t * P:t * P + P], ident[:])
                        last.then_inc(zt_done, 1)

            @block.scalar
            def _(act):
                act.sem_inc(c_xt_kept, XT_START)
                for g in range(2):
                    with act.Fori(0, GB // 2) as k:
                        for par in range(2):
                            n = k * 2 + (par + g * GB)
                            act.wait_ge(c_xt_done, n + 1 + XT_DONE_START)
                            if g:
                                act.wait_ge(zt_done, GT)
                            act.activation(q_g[:, :, ds(k * (2 * T) + par * T, T)], ps_y[par][:, :, 0:T], ACT.Copy)\
                                .then_inc(c_xt_kept, 1)
                    if g == 0:
                        act.dma_start(x_res[:, GT:NT, :], x1_tiles[:, GT:NT, :]).then_inc(x1_load[1], 16)

            @block.vector
            def _(dve):
                dve.sem_inc(prods_ready, PRODS_START)
                dve.sem_inc(x2_ready, X2_START)
                dve.sem_inc(z_ready, Z_START)

                def row(tile, t):
                    return tile[:, ds(t, 1), :].rearrange("p o e -> p (o e)")

                def normalise(g, k, par):
                    n = k * 2 + (par + g * GB)
                    dve.wait_ge(c_xt_done, n + (1 - 2 + XT_DONE_START))
                    for tt in range(TT):
                        t = n * TT + tt
                        dve.tensor_scalar(xn_g[par][:, tt, :], row(x_res, t), all_moments[:, ds(t, 1), 0], all_rstd[:, ds(t, 1)],
                                          ALU.subtract, ALU.mult).then_inc(c_xn, 1)

                def multiply(g, k, par):
                    h, own = k * 2 + (par + g * SH), k * 2 + par
                    dve.wait_ge(y_ready, h + (1 + Y_START))
                    dve.wait_ge(z_ready, h + (1 - 2 + Z_START))
                    y = ps_y[par][:, :, 0:GB * PAIRS].rearrange("p c (b q) -> p c b q", b=GB)
                    for col, i, j, n in pair_segments():
                        d = col // SD
                        uses = [(i, j, d)]
                        if d == SD // 2:
                            uses += [(j, i, d)]
                        elif d:
                            uses += [(j, i, SD // 2 + d)]
                        for to, q_from, term in uses:
                            last = dve.tensor_tensor(prods[par][:, :, :, to:to + n, term], y[:, :, :, col:col + n],
                                                     head_of(q_g, own, q_from, n), ALU.mult)
                    last.then_inc(prods_ready, 1)

                def add_up(g, k, par):
                    wait_apart(dve, folded, k * 2 + (par + g * SH + 1), passed)
                    dve.tensor_reduce(head_of(q_g, k * 2 + par, 0, SD), prods[par][:, :, :, :, 0:SD - FOLD], AX_X,
                                      ALU.add).then_inc(z_ready, 1)

                dve.wait_ge(x1_rstd, 1)
                for g in range(2):
                    dve.wait_ge(x1_load[g], 16)
                    if g:
                        dve.wait_ge(c_rstd, 1)
                    with dve.Fori(0, GB // 2) as k:
                        for par in range(2):
                            normalise(g, k, par)
                    if g:
                        dve.wait_ge(x2_ready, GT + X2_START)
                        for t in range(GT + 1):
                            if t < GT:
                                dve.bn_stats(all_stats[:, t, :], x_res[:, t, :]).then_inc(x2_stats, 1)
                            if t:
                                dve.wait_ge(x2_stats, t)
                                dve.bn_aggr(all_moments[:, t - 1, :], all_stats[:, t - 1, :]).then_inc(x2_moments, 1)
                    dve.wait_ge(c_xt_kept, (g + 1) * GB + XT_START)
                    multiply(g, 0, 0)
                    multiply(g, 0, 1)
                    add_up(g, 0, 0)
                    with dve.Fori(1, SH // 2) as k:
                        multiply(g, k, 0)
                        add_up(g, k - 1, 1)
                        multiply(g, k, 1)
                        add_up(g, k, 0)
                    add_up(g, SH // 2 - 1, 1)
                    for t in range(GT):
                        n = g * GT + t
                        dve.wait_ge(zt_done, n + 1)
                        dve.tensor_tensor(x_res[:, n, :], ps_y[t % 8 // EC][:, t % EC, :], x_res[:, n, :],
                                          ALU.add).then_inc(x2_ready, 1)


        BATCH = 4
        N_BATCHES = NT // BATCH
        ROUNDS = N_BATCHES // 2
        RING = 8
        BUFS = 4
        AHEAD = 3
        FC = FI // P
        ROUTE_OPS = 24
        assert NE == 8 and N_TILES % RING == 0 and N_BATCHES % 2 == 0 and ROUNDS >= 2 and RING == 2 * BUFS

        with ExitStack() as scope:
            def sb(name, shape, dt=F32):
                return sbuf(name, shape, dt, scope)

            w_gu_lo = sb("w_gu_lo", [P, NE, EC, 2 * FI], F32R)
            w_gu = (w_gu_hi, w_gu_lo)
            w_down = sb("w_down", [P, NE, FC, E])
            w_router = sb("w_router", [P, EC, NE])
            tile_expert_i = sb("tile_expert_i", [P, N_TILES], I32)
            tile_row_i = sb("tile_row_i", [P, N_TILES], I32)

            def sb_in(part, name, shape, dt=F32):
                return sbuf(name, shape, dt, part)

            with ExitStack() as routing:
                xn_c = [sb_in(routing, f"xn_c{i}", [P, E]) for i in range(2 * BATCH)]
                w_half = [sb_in(routing, f"w_half{i}", [P, 2, 2 * FI]) for i in range(2)]
                xt_c = [sb_in(routing, f"xt_c{i}", [P, EC, P]) for i in range(2)]
                backward_i = sb_in(routing, "backward_i", [P, NE], I32)
                backward = sb_in(routing, "backward", [P, NE])
                first_row_i = sb_in(routing, "first_row_i", [P, NE], I32)
                first_row = sb_in(routing, "first_row", [P, NE])
                pair_i = sb_in(routing, "pair_i", [P, NT, TOP, 2], I32)
                pair = sb_in(routing, "pair", [P, NT, TOP, 2])
                ones_b = sb_in(routing, "ones_b", [P, P], BF16)
                before_b = sb_in(routing, "before_b", [P, P], BF16)
                best = [sb_in(routing, f"best{i}", [P, BATCH]) for i in range(TOP)]
                is_best = sb_in(routing, "is_best", [P, BATCH, NE])
                rest = sb_in(routing, "rest", [P, BATCH, NE])
                which = sb_in(routing, "which", [P, BATCH])
                one_hot = sb_in(routing, "one_hot", [P, BATCH, TOP, NE])
                chosen_b = sb_in(routing, "chosen_b", [P, BATCH, NE], BF16)
                ratio = [sb_in(routing, f"ratio{i}", [P, BATCH]) for i in range(2)]
                ratio_sum = sb_in(routing, "ratio_sum", [P, BATCH])
                place = sb_in(routing, "place", [P, BATCH, NE])
                place_of = sb_in(routing, "place_of", [P, BATCH, TOP, NE])
                position = sb_in(routing, "position", [P, BATCH, TOP])
                batch_sum = sb_in(routing, "batch_sum", [P, NE])
                lane_sum = sb_in(routing, "lane_sum", [P, NE])
                lane_sum_b = sb_in(routing, "lane_sum_b", [P, NE], BF16)
                pair_rows = [sb_in(routing, f"pair_rows{i}", [P, BATCH, TOP, PAIR_ROW]) for i in range(2)]
                dest = [sb_in(routing, f"dest{i}", [P, BATCH, TOP], U32) for i in range(2)]
                tiles_i = sb_in(routing, "tiles_i", [P, NE], I32)
                tiles_f = sb_in(routing, "tiles_f", [P, NE])
                tile_end = sb_in(routing, "tile_end", [P, NE])
                ones_f = sb_in(routing, "ones_f", [P, NE])
                tile_iota_i = sb_in(routing, "tile_iota_i", [P, N_TILES], I32)
                tile_iota = sb_in(routing, "tile_iota", [P, N_TILES])
                tile_past = sb_in(routing, "tile_past", [P, N_TILES, NE])
                tile_expert = sb_in(routing, "tile_expert", [P, N_TILES])
                tile_start = sb_in(routing, "tile_start", [P, N_TILES])
            with ExitStack() as tiling:
                pair_row = [sb_in(tiling, f"pair_row{i}", [P, PAIR_ROW]) for i in range(RING)]
                take = [sb_in(tiling, f"take{i}", [P, 1], U32) for i in range(RING)]
                back = [sb_in(tiling, f"back{i}", [P, 1], U32) for i in range(RING)]
                srow = [sb_in(tiling, f"srow{i}", [P, E]) for i in range(BUFS)]
                st = [[sb_in(tiling, f"st_{part}{i}", [P, EC, P], F32R) for part in ("hi", "lo")] for i in range(2)]
                silu_g = [sb_in(tiling, f"silu_g{i}", [P, FI]) for i in range(2)]
                hidden = [sb_in(tiling, f"hidden{i}", [P, FI]) for i in range(2)]
                hidden_t = [sb_in(tiling, f"hidden_t{i}", [P, FC, P]) for i in range(2)]
                y_row = [sb_in(tiling, f"y_row{i}", [P, E]) for i in range(BUFS)]

            ps_x = psum("ps_x", [P, 2, E], scope)
            ps_gu = psum("ps_gu", [P, 2, 2 * FI], scope)
            ps_ht = psum("ps_ht", [P, E], scope)
            ps_down = psum("ps_down", [P, 2, E], scope)
            ps_count = psum("ps_count", [P, E], scope)
            ps_logit = [ps_gu[:, i, :] for i in range(2)]
            ps_rank = ps_ht

            router_load = sem("router_load")
            w_load = sem("w_load")
            w_half_load = [sem(f"w_half_load{i}") for i in range(2)]
            w_gu_hi_ready = sem("w_gu_hi_ready")
            w_gu_ready = [sem(f"w_gu_ready{i}") for i in range(2)]
            m_consts = sem("m_consts")
            m_rstd_step = sem("m_rstd_step")
            m_rstd = sem("m_rstd")
            m_stats = sem("m_stats")
            m_moments = sem("m_moments")
            n_ready = sem("n_ready")
            n_stored = [sem(f"n_stored{i}") for i in range(2 * BATCH)]
            nt_done = sem("nt_done")
            nt_kept = sem("nt_kept")
            logits_done = sem("logits_done")
            logits_read = sem("logits_read")
            const_step = sem("const_step")
            route = sem("route")
            gap_ready = sem("gap_ready")
            ratio_ready = sem("ratio_ready")
            chosen_ready = sem("chosen_ready")
            ranked = sem("ranked")
            pair_rows_ready = sem("pair_rows_ready")
            pairs_scattered = [sem(f"pairs_scattered{i}") for i in range(2)]
            summed = sem("summed")
            counted = sem("counted")
            list_step = sem("list_step")
            tiles_known = sem("tiles_known")
            pair_load = [sem(f"pair_load{i}") for i in range(RING)]
            take_ready = sem("take_ready")
            row_load = [sem(f"row_load{i}") for i in range(BUFS)]
            st_done = sem("st_done")
            st_hi_kept = sem("st_hi_kept")
            st_lo_kept = sem("st_lo_kept")
            gu_done = sem("gu_done")
            silu_ready = sem("silu_ready")
            hidden_ready = sem("hidden_ready")
            ht_done = sem("ht_done")
            ht_kept = sem("ht_kept")
            down_done = sem("down_done")
            y_ready = sem("y_row_ready")
            y_scattered = [sem(f"y_scattered{i}") for i in range(BUFS)]
            x2_stored = sem("x2_stored")
            NT_START, ST_LO_START, HIDDEN_START, DOWN_START, Y_START, KEPT_START = 2, 2, 2, 2, 2, 1

            xn_view = xn_rows.rearrange("(t p) e -> p t e", p=P)
            out_rows = out.rearrange("b t e -> (b t) e")
            X2_STORES = NE
            assert NT == NE * BATCH and 2 * FI == E

            def row(tile, t):
                return tile[:, ds(t, 1), :].rearrange("p o e -> p (o e)")

            def first_round(k):
                return isinstance(k, int) and k == 0

            def rounds(eng, n, per_round, emit):
                for k in (0, None, n - 1):
                    if k is None and n == 2:
                        pass
                    elif k is None:
                        with eng.Fori(1, n - 1) as k:
                            for r in range(per_round):
                                emit(k, r, False)
                    else:
                        for r in range(per_round):
                            emit(k, r, k == n - 1)

            def route_steps(eng, emit):
                rounds(eng, ROUNDS, 2, lambda k, par, last: emit(k, par, last and par == 1))

            def batch_after(k, par):
                return (k, 1) if par == 0 else (k + 1, 0)

            def batch_before(k, par):
                return (k, 0) if par == 1 else (k - 1, 1)

            def batch_no(k, par):
                return k * 2 + par

            def tile_steps(eng, emit):
                rounds(eng, N_TILES // RING, RING, emit)

            def at(kk, r, ahead=0):
                return (kk + 1, r + ahead - RING) if r + ahead >= RING else (kk, r + ahead)

            def exists(last, r, ahead):
                return not (last and r + ahead >= RING)

            def tile_no(kk, r):
                return kk * RING + r

            def split_lo(eng, half, e):
                lo, hi = [w[:, ds(e, 1), 2 * half:2 * half + 2, :].rearrange("p o c f -> p (o c) f")
                          for w in (w_gu_lo, w_gu_hi)]
                eng.tensor_tensor(lo, w_half[half][:], hi, ALU.subtract).then_inc(w_gu_ready[half], 1)

            def turn(kk, r):
                return kk * (RING // BUFS) + r // BUFS

            block = scope.enter_context(nc.Block())

            @block.sync
            def _(sp):
                sp.dma_start(w_router[:], router_t.rearrange("(c p) n -> p c n", p=P)).then_inc(router_load, 16)
                for e in range(NE):
                    sp.wait_ge(n_ready, e * (NT // NE) + 1)
                    if e:
                        sp.wait_ge(x2_stored, e * 16)
                    tiles = slice(e * (NT // X2_STORES), (e + 1) * (NT // X2_STORES))
                    sp.dma_start(out_tiles[:, tiles, :], x_res[:, tiles, :]).then_inc(x2_stored, 16)
                    sp.dma_start(w_down[:, e, :, :], down[e].rearrange("(c p) n -> p c n", p=P)).then_inc(w_load, 16)
                    for half in range(2):
                        if e:
                            sp.wait_ge(w_gu_ready[half], e)
                        sp.dma_start(w_half[half][:], gate_up[e].rearrange("(h c p) g f -> h p c (g f)", h=2, p=P)[half])\
                          .then_inc(w_half_load[half], 16)
                sp.wait_ge(tiles_known, 1)
                for par in range(2):
                    sp.wait_ge(pairs_scattered[par], ROUNDS * BATCH * TOP * 16)
                for i in range(2 * BATCH):
                    sp.wait_ge(n_stored[i], ROUNDS * 16)

                def load_pairs(kk, r, last):
                    n = tile_no(kk, r)
                    if not first_round(kk):
                        wait_apart(sp, y_ready, n + 1 - RING + Y_START, passed)
                        wait_apart(sp, pair_load[r], kk * 16, passed)
                    first = sp.value_load(tile_row_i[0:1, ds(n, 1)], min_val=0, max_val=TABLE_ROWS - P)
                    sp.dma_start(pair_row[r][:], row_table[ds(first, P), :]).then_inc(pair_load[r], 16)

                tile_steps(sp, load_pairs)
                for i in range(BUFS):
                    sp.wait_ge(y_scattered[i], N_TILES // BUFS * 16)

            @block.gpsimd
            def _(pool):
                pool.iota(backward_i[:], pattern=[[-1, NE]], base=NE, channel_multiplier=0).then_inc(m_consts, 1)
                pool.iota(first_row_i[:], pattern=[[N_TOK, NE]], base=0, channel_multiplier=0).then_inc(m_consts, 1)
                for s in range(TOP):
                    pool.iota(pair_i[:, :, s, TOKEN], pattern=[[P, NT]], base=0, channel_multiplier=1).then_inc(m_consts, 1)
                    pool.iota(pair_i[:, :, s, BACK], pattern=[[P, NT]], base=0, channel_multiplier=1)\
                        .then_inc(m_consts, 1)
                pool.iota(tile_iota_i[:], pattern=[[1, N_TILES]], base=0, channel_multiplier=0).then_inc(m_consts, 1)
                pool.memset(ones_b[:], 1.0).then_inc(m_consts, 1)
                pool.memset(ones_f[:], 1.0).then_inc(m_consts, 1)
                pool.memset(lane_sum[:], 0.0).then_inc(m_consts, 1)
                pool.memset(lane_sum_b[:], 0.0).then_inc(m_consts, 1)
                for par in range(2):
                    pool.memset(pair_rows[par][:], 0.0).then_inc(m_consts, 1)
                pool.wait_ge(m_consts, 13)
                pool.affine_select(out=before_b[:], in_=ones_b[:], compare_op=ALU.is_gt, fill=0.0, base=0,
                                   pattern=[[1, P]], channel_multiplier=-1).then_inc(m_consts, 1)
                pool.wait_ge(m_moments, GT)
                reciprocal_sqrt(pool, all_rstd[:, GT:NT], all_moments[:, GT:NT, 1], var_eps[:, GT:NT], newton[:, GT:NT],
                                m_rstd_step, 0, m_rstd, passed)

                def scatter_pairs(k, par, last):
                    wait_apart(pool, pair_rows_ready, batch_no(k, par) + 1, passed)
                    for i in range(BATCH):
                        for s in range(TOP):
                            pool.indirect_dma_start(
                                out=row_table[:, :], out_offset=bass.IndirectOffsetOnAxis(ap=dest[par][:, i, s:s + 1], axis=0),
                                in_=pair_rows[par][:, i, s, :], in_offset=None, bounds_check=TABLE_ROWS - 1,
                                oob_is_err=False).then_inc(pairs_scattered[par], 16)

                def route_step(k, par, last):
                    if not (first_round(k) and par == 0):
                        e = batch_no(*batch_before(k, par))
                        wait_apart(pool, w_gu_hi_ready, e * 2 + 2, passed)
                        split_lo(pool, 1, e)
                    scatter_pairs(k, par, last)

                route_steps(pool, route_step)
                pool.wait_ge(w_gu_hi_ready, 2 * NE)
                split_lo(pool, 1, NE - 1)

                def gather(kk, r):
                    n = tile_no(kk, r)
                    wait_apart(pool, take_ready, n + 1, passed)
                    if not (first_round(kk) and r < BUFS):
                        wait_apart(pool, st_done, n + 1 - BUFS, passed)
                    pool.indirect_dma_start(
                        out=srow[r % BUFS][:], out_offset=None, in_=xn_rows[:, :],
                        in_offset=bass.IndirectOffsetOnAxis(ap=take[r][:, 0:1], axis=0), bounds_check=N_TOK - 1,
                        oob_is_err=False).then_inc(row_load[r % BUFS], 16)

                def tile_step(kk, r, last):
                    if exists(last, r, AHEAD):
                        gather(*at(kk, r, AHEAD))
                    wait_apart(pool, y_ready, tile_no(kk, r) + 1 + Y_START, passed)
                    if not (first_round(kk) and r == 0):
                        wait_apart(pool, y_scattered[(r - 1) % BUFS], turn(kk, r - 1) * 16 + 16, passed)
                    pool.indirect_dma_start(
                        out=out_rows, out_offset=bass.IndirectOffsetOnAxis(ap=back[r][:, 0:1], axis=0),
                        in_=y_row[r % BUFS][:], in_offset=None, bounds_check=N_TOK - 1,
                        oob_is_err=False, compute_op=ALU.add).then_inc(y_scattered[r % BUFS], 16)

                for i in range(2 * BATCH):
                    pool.wait_ge(n_stored[i], ROUNDS * 16)
                for r in range(AHEAD):
                    gather(0, r)
                pool.wait_ge(x2_stored, X2_STORES * 16)
                tile_steps(pool, tile_step)

            @block.tensor
            def _(pe):
                pe.sem_inc(down_done, DOWN_START)

                def n_transposes(k, par, i):
                    t = batch_no(k, par) * BATCH + i
                    pe.wait_ge(n_ready, t + 1)
                    pe.wait_ge(nt_kept, t + 1 - 2 + NT_START)
                    for c in range(EC):
                        last = pe.transpose(ps_x[:, i % 2, c * P:c * P + P], xn_c[par * BATCH + i][:, c * P:c * P + P],
                                            ident[:])
                    last.then_inc(nt_done, 1)

                def logits(k, par, i):
                    t = batch_no(k, par) * BATCH + i
                    pe.wait_ge(nt_kept, t + 1 + NT_START)
                    if i == 0 and not first_round(k):
                        pe.wait_ge(logits_read, batch_no(k, par) - 1)
                    for c in range(EC):
                        last = pe.matmul(ps_logit[par][:, i * NE:i * NE + NE], xt_c[i % 2][:, c, :], w_router[:, c, :],
                                         start=(c == 0), stop=(c == EC - 1))
                    if i == BATCH - 1:
                        last.then_inc(logits_done, 1)

                def rank(k, par):
                    pe.wait_ge(chosen_ready, batch_no(k, par) + 1)
                    cols = BATCH * NE
                    pe.matmul(ps_rank[:, 0:cols], before_b[:], chosen_b[:, :, :], start=True, stop=False)
                    for d in range(1, BATCH):
                        pe.matmul(ps_rank[:, d * NE:cols], ones_b[:], chosen_b[:, 0:BATCH - d, :], start=False, stop=False)
                    pe.matmul(ps_rank[:, 0:cols], ones_b[:], lane_sum_b[:].unsqueeze(1).to_broadcast([P, BATCH, NE]),
                              start=False, stop=True).then_inc(ranked, 1)

                def route_step(k, par, last):
                    for i in range(BATCH):
                        if i + 1 < BATCH:
                            n_transposes(k, par, i + 1)
                        elif not last:
                            n_transposes(*batch_after(k, par), 0)
                        logits(k, par, i)
                        if i == 1 and not (first_round(k) and par == 0):
                            rank(*batch_before(k, par))
                    if last:
                        rank(k, par)

                pe.wait_ge(router_load, 16)
                pe.wait_ge(m_consts, 14)
                n_transposes(0, 0, 0)
                route_steps(pe, route_step)
                pe.wait_ge(summed, N_BATCHES)
                pe.matmul(ps_count[:, 0:NE], ones_b[:], lane_sum_b[:], start=True, stop=True).then_inc(counted, 1)

                def s_transposes(kk, r):
                    n = tile_no(kk, r)
                    pe.wait_ge(row_load[r % BUFS], turn(kk, r) * 16 + 16)
                    pe.wait_ge(st_lo_kept, n + 1 - 2 + ST_LO_START)
                    for c in range(EC):
                        last = pe.transpose(ps_x[:, r % 2, c * P:c * P + P], srow[r % BUFS][:, c * P:c * P + P], ident[:])
                    last.then_inc(st_done, 1)

                def expert(kk, r):
                    return pe.value_load(tile_expert_i[0:1, ds(tile_no(kk, r), 1)], min_val=0, max_val=NE - 1)

                def gate_and_up(kk, r, e):
                    n = tile_no(kk, r)
                    pe.wait_ge(st_lo_kept, n + 1 + ST_LO_START)
                    pe.wait_ge(hidden_ready, n + 1 - 2 + HIDDEN_START)
                    for c in range(EC):
                        for x_part, w_part in ((0, 0), (0, 1), (1, 0)):
                            last = pe.matmul(ps_gu[:, r % 2, :], st[r % 2][x_part][:, c, :],
                                             w_gu[w_part][:, ds(e, 1), c, :].rearrange("p o f -> p (o f)"),
                                             start=(c == 0 and w_part == x_part == 0), stop=(c == EC - 1 and x_part == 1))
                    last.then_inc(gu_done, 1)

                def h_transposes(kk, r):
                    n = tile_no(kk, r)
                    pe.wait_ge(hidden_ready, n + 1 + HIDDEN_START)
                    pe.wait_ge(ht_kept, n + KEPT_START)
                    for c in range(FC):
                        last = pe.transpose(ps_ht[:, c * P:c * P + P], hidden[r % 2][:, c * P:c * P + P], ident[:])
                    last.then_inc(ht_done, 1)

                def down_rows(kk, r, e):
                    n = tile_no(kk, r)
                    pe.wait_ge(ht_kept, n + 1 + KEPT_START)
                    pe.wait_ge(y_ready, n + 1 - 2 + Y_START)
                    for c in range(FC):
                        last = pe.matmul(ps_down[:, r % 2, :], hidden_t[r % 2][:, c, :],
                                         w_down[:, ds(e, 1), c, :].rearrange("p o f -> p (o f)"),
                                         start=(c == 0), stop=(c == FC - 1))
                    last.then_inc(down_done, 1)

                def tile_step(kk, r, last):
                    e = expert(kk, r)
                    if exists(last, r, 1):
                        e_next = expert(*at(kk, r, 1))
                    if exists(last, r, 2):
                        s_transposes(*at(kk, r, 2))
                    h_transposes(kk, r)
                    if exists(last, r, 1):
                        gate_and_up(*at(kk, r, 1), e_next)
                    down_rows(kk, r, e)

                pe.wait_ge(w_load, 16 * NE)
                for half in range(2):
                    pe.wait_ge(w_gu_ready[half], NE)
                pe.wait_ge(tiles_known, 1)
                s_transposes(0, 0)
                s_transposes(0, 1)
                gate_and_up(0, 0, expert(0, 0))
                tile_steps(pe, tile_step)

            @block.scalar
            def _(act):
                act.sem_inc(nt_kept, NT_START)
                act.sem_inc(y_ready, Y_START)

                def split_hi(e):
                    act.wait_ge(x2_stored, e * 16 + 16)
                    for half in range(2):
                        act.wait_ge(w_half_load[half], e * 16 + 16)
                        act.activation(w_gu_hi[:, ds(e, 1), 2 * half:2 * half + 2, :].rearrange("p o c f -> p (o c) f"),
                                       w_half[half][:], ACT.Copy).then_inc(w_gu_hi_ready, 1)

                def score_ratio(k, par):
                    act.wait_ge(gap_ready, batch_no(k, par) + 1)
                    act.activation(ratio[par][:], ratio[par][:], ACT.Exp).then_inc(ratio_ready, 1)

                def route_step(k, par, last):
                    for i in range(BATCH):
                        t = batch_no(k, par) * BATCH + i
                        buf = par * BATCH + i
                        act.wait_ge(n_ready, t + 1)
                        if not first_round(k):
                            act.wait_ge(n_stored[buf], k * 16)
                        act.dma_start(xn_view[:, ds(t, 1), :], xn_c[buf][:].unsqueeze(1)).then_inc(n_stored[buf], 16)
                        act.wait_ge(nt_done, t + 1)
                        act.activation(xt_c[i % 2][:], ps_x[:, i % 2, :], ACT.Copy).then_inc(nt_kept, 1)
                        if i == 1 and not (first_round(k) and par == 0):
                            score_ratio(*batch_before(k, par))
                    if not first_round(k):
                        split_hi(batch_no(k - 1, par))
                    if last:
                        score_ratio(k, par)
                        split_hi(NE - 2)
                        split_hi(NE - 1)

                route_steps(act, route_step)

                def keep_st(kk, r):
                    act.wait_ge(st_done, tile_no(kk, r) + 1)
                    act.activation(st[r % 2][0][:], ps_x[:, r % 2, :], ACT.Copy).then_inc(st_hi_kept, 1)

                def silu_of(kk, r):
                    n = tile_no(kk, r)
                    act.wait_ge(gu_done, n + 1)
                    act.wait_ge(hidden_ready, n + 1 - 2 + HIDDEN_START)
                    act.activation(silu_g[r % 2][:], ps_gu[:, r % 2, 0:FI], ACT.Silu).then_inc(silu_ready, 1)

                def weigh(kk, r):
                    n = tile_no(kk, r)
                    act.wait_ge(down_done, n + 1 + DOWN_START)
                    if not (first_round(kk) and r < BUFS):
                        act.wait_ge(y_scattered[r % BUFS], turn(kk, r) * 16)
                    act.activation(y_row[r % BUFS][:], ps_down[:, r % 2, :], ACT.Copy,
                                   scale=pair_row[r][:, SCORE:SCORE + 1]).then_inc(y_ready, 1)

                def tile_step(kk, r, last):
                    if exists(last, r, 2):
                        keep_st(*at(kk, r, 2))
                    if exists(last, r, 1):
                        silu_of(*at(kk, r, 1))
                    weigh(kk, r)

                keep_st(0, 0)
                keep_st(0, 1)
                silu_of(0, 0)
                tile_steps(act, tile_step)

            @block.vector
            def _(dve):
                dve.sem_inc(hidden_ready, HIDDEN_START)
                dve.sem_inc(ht_kept, KEPT_START)
                dve.sem_inc(st_lo_kept, ST_LO_START)

                def n_rows(k, par):
                    for i in range(BATCH):
                        t = batch_no(k, par) * BATCH + i
                        buf = par * BATCH + i
                        if not first_round(k):
                            dve.wait_ge(nt_done, t + 1 - 2 * BATCH)
                            dve.wait_ge(n_stored[buf], k * 16)
                        dve.tensor_scalar(xn_c[buf][:], row(x_res, t), all_moments[:, ds(t, 1), 0], all_rstd[:, ds(t, 1)],
                                          ALU.subtract, ALU.mult).then_inc(n_ready, 1)

                def route_batch(k, par):
                    b = batch_no(k, par)
                    steps = [0]

                    def chain(instruction):
                        steps[0] += 1
                        instruction.then_inc(route, 1)
                        wait_apart(dve, route, b * ROUTE_OPS + steps[0], passed)

                    def by_token(tile):
                        return tile[:].unsqueeze(2).to_broadcast([P, BATCH, NE])

                    logit = ps_logit[par][:, 0:BATCH * NE].rearrange("p (t n) -> p t n", n=NE)
                    numbers = backward[:].unsqueeze(1).to_broadcast([P, BATCH, NE])
                    wait_apart(dve, logits_done, b + 1, passed)
                    for s, values in enumerate((logit, rest[:])):
                        chain(dve.tensor_reduce(best[s][:], values, AX_X, ALU.max))
                        chain(dve.tensor_tensor(is_best[:], values, by_token(best[s]), ALU.is_equal))
                        chain(dve.tensor_tensor(is_best[:], is_best[:], numbers, ALU.mult))
                        chain(dve.tensor_reduce(which[:], is_best[:], AX_X, ALU.max))
                        chain(dve.tensor_tensor(one_hot[:, :, s, :], numbers, by_token(which), ALU.is_equal))
                        if s == 0:
                            chain(dve.scalar_tensor_tensor(rest[:], one_hot[:, :, 0, :], -3.0e38, logit, ALU.mult, ALU.add))
                            dve.sem_inc(logits_read, 1)
                    dve.tensor_tensor(chosen_b[:], one_hot[:, :, 0, :], one_hot[:, :, 1, :], ALU.add).then_inc(chosen_ready, 1)
                    dve.tensor_tensor(ratio[par][:], best[1][:], best[0][:], ALU.subtract).then_inc(gap_ready, 1)
                    if not first_round(k):
                        wait_apart(dve, pairs_scattered[par], k * (BATCH * TOP * 16), passed)
                    def run(instruction):
                        steps[0] += 1
                        instruction.then_inc(route, 1)
                        return steps[0]

                    def need(operation):
                        wait_apart(dve, route, b * ROUTE_OPS + operation, passed)

                    run(dve.tensor_copy(pair_rows[par][:, :, :, 0:2], pair[:, ds(b * BATCH, BATCH), :, :]))
                    wait_apart(dve, ratio_ready, b + 1, passed)
                    added = run(dve.tensor_scalar(ratio_sum[:], ratio[par][:], 1.0, None, ALU.add))
                    wait_apart(dve, ranked, b + 1, passed)
                    placed = run(dve.tensor_tensor(place[:], ps_rank[:, 0:BATCH * NE].rearrange("p (t n) -> p t n", n=NE),
                                                   first_row[:].unsqueeze(1).to_broadcast([P, BATCH, NE]), ALU.add))
                    need(added)
                    first_score = run(dve.reciprocal(pair_rows[par][:, :, 0, SCORE], ratio_sum[:]))
                    need(placed)
                    for s in range(TOP):
                        picked = run(dve.tensor_tensor(place_of[:, :, s, :], place[:], one_hot[:, :, s, :], ALU.mult))
                    need(first_score)
                    run(dve.tensor_tensor(pair_rows[par][:, :, 1, SCORE], ratio[par][:], pair_rows[par][:, :, 0, SCORE],
                                          ALU.mult))
                    need(picked)
                    positioned = run(dve.tensor_reduce(position[:], place_of[:], AX_X, ALU.add))
                    in_batch = run(dve.tensor_reduce(batch_sum[:], chosen_b[:].rearrange("p t n -> p n t"), AX_X, ALU.add))
                    need(positioned)
                    destined = run(dve.tensor_copy(dest[par][:], position[:]))
                    need(in_batch)
                    in_all = run(dve.tensor_tensor(lane_sum[:], lane_sum[:], batch_sum[:], ALU.add))
                    need(destined)
                    dve.sem_inc(pair_rows_ready, 1)
                    need(in_all)
                    need(run(dve.tensor_copy(lane_sum_b[:], lane_sum[:])))
                    dve.sem_inc(summed, 1)
                    assert steps[0] <= ROUTE_OPS
                    dve.sem_inc(route, ROUTE_OPS - steps[0])

                def route_step(k, par, last):
                    if not last:
                        n_rows(k + 1, par)
                    route_batch(k, par)
                    if not (first_round(k) and par == 0):
                        e = batch_no(*batch_before(k, par))
                        dve.wait_ge(w_gu_hi_ready, e * 2 + 1)
                        split_lo(dve, 0, e)

                n_rows(0, 0)
                n_rows(0, 1)
                for t in range(GT, NT + 1):
                    if t < NT:
                        dve.bn_stats(all_stats[:, t, :], x_res[:, t, :]).then_inc(m_stats, 1)
                    if t > GT:
                        dve.wait_ge(m_stats, t - GT)
                        dve.bn_aggr(all_moments[:, t - 1, :], all_stats[:, t - 1, :]).then_inc(m_moments, 1)
                dve.wait_ge(m_consts, 14)
                for n, (to, of) in enumerate(((backward, backward_i), (first_row, first_row_i), (pair, pair_i),
                                              (tile_iota, tile_iota_i))):
                    dve.tensor_copy(to[:], of[:]).then_inc(const_step, 1)
                dve.wait_ge(const_step, 4)
                dve.wait_ge(m_rstd, 1)
                rounds(dve, ROUNDS, 2, route_step)

                step = [0]

                def chain(instruction):
                    step[0] += 1
                    instruction.then_inc(list_step, 1)
                    dve.wait_ge(list_step, step[0])

                dve.wait_ge(counted, 1)
                chain(dve.tensor_scalar(tiles_i[:], ps_count[:, 0:NE], float(P - 1), None, ALU.add))
                chain(dve.tensor_scalar(tiles_i[:], tiles_i[:], 7, None, ALU.arith_shift_right))
                chain(dve.tensor_copy(tiles_f[:], tiles_i[:]))
                chain(dve.tensor_tensor_scan(tile_end[:], ones_f[:], tiles_f[:], 0.0, ALU.mult, ALU.add))
                chain(dve.tensor_tensor(tile_past[:], tile_iota[:].unsqueeze(2).to_broadcast([P, N_TILES, NE]),
                                        tile_end[:].unsqueeze(1).to_broadcast([P, N_TILES, NE]), ALU.is_ge))
                chain(dve.tensor_reduce(tile_expert[:], tile_past[:], AX_X, ALU.add))
                chain(dve.tensor_tensor(tile_past[:], tile_past[:], tiles_f[:].unsqueeze(1).to_broadcast([P, N_TILES, NE]),
                                        ALU.mult))
                chain(dve.tensor_reduce(tile_start[:], tile_past[:], AX_X, ALU.add))
                chain(dve.tensor_tensor(tile_iota[:], tile_iota[:], tile_start[:], ALU.subtract))
                chain(dve.tensor_scalar(tile_iota[:], tile_iota[:], float(P), None, ALU.mult))
                chain(dve.scalar_tensor_tensor(tile_start[:], tile_expert[:], float(N_TOK), tile_iota[:], ALU.mult, ALU.add))
                chain(dve.tensor_copy(tile_row_i[:], tile_start[:]))
                chain(dve.tensor_scalar(tile_expert[:], tile_expert[:], float(NE - 1), None, ALU.min))
                dve.tensor_copy(tile_expert_i[:], tile_expert[:]).then_inc(tiles_known, 1)
                dve.wait_ge(w_gu_hi_ready, 2 * NE - 1)
                split_lo(dve, 0, NE - 1)

                def read_pairs(kk, r):
                    n = tile_no(kk, r)
                    dve.wait_ge(pair_load[r], kk * 16 + 16)
                    if not first_round(kk):
                        dve.wait_ge(y_scattered[r % BUFS], turn(kk, r) * 16 - 16)
                    dve.tensor_copy(take[r][:], pair_row[r][:, TOKEN:TOKEN + 1])
                    dve.tensor_copy(back[r][:], pair_row[r][:, BACK:BACK + 1]).then_inc(take_ready, 1)

                def keep_ht(kk, r):
                    n = tile_no(kk, r)
                    dve.wait_ge(ht_done, n + 1)
                    dve.wait_ge(down_done, n + 1 - 2 + DOWN_START)
                    dve.tensor_copy(hidden_t[r % 2][:].rearrange("p c t -> p (c t)"), ps_ht[:, 0:FI]).then_inc(ht_kept, 1)

                def gated(kk, r):
                    dve.wait_ge(silu_ready, tile_no(kk, r) + 1)
                    dve.tensor_tensor(hidden[r % 2][:], ps_gu[:, r % 2, FI:2 * FI], silu_g[r % 2][:], ALU.mult)\
                       .then_inc(hidden_ready, 1)

                def keep_st_lo(kk, r):
                    dve.wait_ge(st_hi_kept, tile_no(kk, r) + 1)
                    dve.tensor_tensor(st[r % 2][1][:].rearrange("p c t -> p (c t)"), ps_x[:, r % 2, :],
                                      st[r % 2][0][:].rearrange("p c t -> p (c t)"), ALU.subtract).then_inc(st_lo_kept, 1)

                def tile_step(kk, r, last):
                    if exists(last, r, 2):
                        keep_st_lo(*at(kk, r, 2))
                    keep_ht(kk, r)
                    if exists(last, r, AHEAD + 1):
                        read_pairs(*at(kk, r, AHEAD + 1))
                    if exists(last, r, 1):
                        gated(*at(kk, r, 1))

                for r in range(AHEAD + 1):
                    read_pairs(0, r)
                keep_st_lo(0, 0)
                keep_st_lo(0, 1)
                gated(0, 0)
                tile_steps(dve, tile_step)


def kernel(x, ctx_2048, L0_attn_Wq, L0_attn_bq, L0_attn_Wk, L0_attn_bk, L0_attn_Wv, L0_attn_bv,
           L0_attn_Wo, L0_attn_bo, L0_attn_slopes, L0_xattn_ssm_kernel, L0_xattn_D,
           L0_ffn_router_gate, L0_ffn_expert_gate_up, L0_ffn_expert_down):
    import numpy as np
    import concourse.bacc as bacc
    from concourse.bass_utils import run_bass_kernel_spmd

    B, T, E = x.shape
    n_experts, _, two_f = L0_ffn_expert_gate_up.shape
    laid_out = {
        "x": x,
        "ctx_t": np.transpose(ctx_2048, (2, 0, 1)).reshape(E // P, P, B * T)[:, ::-1].reshape(E, B * T),
        "wq_t": np.transpose(L0_attn_Wq), "bq": np.transpose(np.reshape(L0_attn_bq, (E // P, P))),
        "wk_t": np.transpose(L0_attn_Wk), "bk": np.transpose(np.reshape(L0_attn_bk, (E // P, P))),
        "wv_t": np.transpose(L0_attn_Wv), "bv": L0_attn_bv,
        "wo_t": np.transpose(L0_attn_Wo), "bo": L0_attn_bo,
        "slopes": L0_attn_slopes,
        "ssm_kernel": L0_xattn_ssm_kernel, "ssm_d": L0_xattn_D,
        "router_t": np.transpose(L0_ffn_router_gate),
        "gate_up": np.transpose(np.reshape(L0_ffn_expert_gate_up, (n_experts, E, two_f // 2, 2)), (0, 1, 3, 2)),
        "down": L0_ffn_expert_down,
    }
    nc = bacc.Bacc("TRN2", target_bir_lowering=False, num_devices=1)
    arrays, args = {}, []
    for name, a in laid_out.items():
        a = np.ascontiguousarray(a)
        arrays[f"in_{name}"] = a
        args.append(nc.dram_tensor(f"in_{name}", a.shape, mybir.dt.from_np(a.dtype), kind="ExternalInput").ap())
    args.append(nc.dram_tensor("out", (B, T, E), F32, kind="ExternalOutput").ap())
    build_decoder(nc, *args)
    r = run_bass_kernel_spmd(nc, [arrays], core_ids=[0])
    return r.results[0]["out"]
```
